# Optimizing a Trainium2 kernel written in Bass

```python
import numpy as np
import jax
import jax.numpy as jnp

def _softmax(x, axis=-1):
    return jax.nn.softmax(x, axis=axis)

def _gelu(x):
    return jax.nn.gelu(x, approximate=True)

def _silu(x):
    return jax.nn.silu(x)

def _sigmoid(x):
    return jax.nn.sigmoid(x)

def _layernorm(x, axis=-1, eps=1e-05):
    m = jnp.mean(x, axis=axis, keepdims=True)
    v = jnp.var(x, axis=axis, keepdims=True)
    return (x - m) / jnp.sqrt(v + eps)

def _scatter_add(tgt, idx, src, axis=0):
    return tgt.at[idx].add(src)

def _segment_sum(src, seg, n):
    return jax.ops.segment_sum(src, seg, n)
kernel_name = 'mk_adj_preln_d2_adj_r2_b6a19b'

def setup_inputs(seed: int=0):
    np.random.seed(seed)
    _w = jnp.asarray

    def _rec_inputs():
        import jax
        import jax.numpy as jnp
        _gk = jax.random.key(seed)
        x = -0.0001538 + 1 * jax.random.normal(jax.random.fold_in(_gk, 1), (64, 128, 384), jnp.float32)
        _a = jax.random.bernoulli(jax.random.fold_in(_gk, 2), 0.0625, (64, 128, 128))
        _a = jnp.logical_or(_a, jnp.swapaxes(_a, -1, -2))
        _a = jnp.logical_or(_a, jnp.eye(128, dtype=bool))
        _af = _a.astype(jnp.float32)
        _af = _af * jax.random.uniform(jax.random.fold_in(_gk, 3), (64, 128, 128), jnp.float32, 0.05, 4.42607)
        adj = _af
        return (x, adj)
    x, adj = _rec_inputs()

    def _L0_gnn_setup():
        import jax, jax.numpy as jnp
        import numpy as np
        NUM_HEADS = 12
        HIDDEN = 384
        HEAD = HIDDEN // NUM_HEADS
        B, N = (16, 256)
        key = jax.random.key(seed)
        ks = jax.random.split(key, 9)
        s = 0.02
        return {'x': jax.random.normal(ks[0], (B, N, HIDDEN), jnp.float32), 'spatial_encoding': jax.random.normal(ks[1], (B, N, N), jnp.float32), 'edge_encoding': jax.random.normal(ks[2], (B, N, N), jnp.float32), 'Wq': jax.random.normal(ks[3], (HIDDEN, HIDDEN), jnp.float32) * s, 'Wk': jax.random.normal(ks[4], (HIDDEN, HIDDEN), jnp.float32) * s, 'Wv': jax.random.normal(ks[5], (HIDDEN, HIDDEN), jnp.float32) * s, 'bv': jax.random.normal(ks[6], (HIDDEN,), jnp.float32) * s, 'Wo': jax.random.normal(ks[7], (HIDDEN, HIDDEN), jnp.float32) * s, 'bo': jax.random.normal(ks[8], (HIDDEN,), jnp.float32) * s}
    _L0_gnn_all = _L0_gnn_setup()
    _L0_gnn_in = {k: v for k, v in _L0_gnn_all.items() if k in ('Wq', 'Wk', 'Wv', 'bv', 'Wo', 'bo')}
    del _L0_gnn_all

    def _L1_gnn_setup():
        import jax, jax.numpy as jnp
        import numpy as np
        B, S, H, L = (32, 256, 384, 2)

        def _layer_norm(z, a, b, eps=0.001):
            mu = jnp.mean(z, axis=-1, keepdims=True)
            sigma = jnp.std(z, axis=-1, keepdims=True, ddof=1)
            return (z - mu) / (sigma + eps) * a + b
        key = jax.random.key(seed)
        ks = jax.random.split(key, 6)
        hidden_state = jax.random.normal(ks[0], (B, S, H), dtype=jnp.float32)
        adjacency_matrix = (jax.random.uniform(ks[1], (B, S, S)) < 0.2).astype(jnp.float32)
        W_left = 0.05 * jax.random.normal(ks[2], (L, H, H), dtype=jnp.float32)
        W_right = 0.05 * jax.random.normal(ks[3], (L, H, H), dtype=jnp.float32)
        W_lin = 0.05 * jax.random.normal(ks[4], (L, H, H), dtype=jnp.float32)
        b_lin = jnp.zeros((L, H), dtype=jnp.float32)
        ln_a = jnp.ones((L, H), dtype=jnp.float32)
        ln_b = jnp.zeros((L, H), dtype=jnp.float32)
        return {'hidden_state': hidden_state, 'adjacency_matrix': adjacency_matrix, 'W_left': W_left, 'W_right': W_right, 'W_lin': W_lin, 'b_lin': b_lin, 'ln_a': ln_a, 'ln_b': ln_b}
    _L1_gnn_all = _L1_gnn_setup()
    _L1_gnn_in = {k: v for k, v in _L1_gnn_all.items() if k in ('W_left', 'W_right', 'W_lin', 'b_lin', 'ln_a', 'ln_b')}
    del _L1_gnn_all
    return {'x': x, 'adj': adj, 'L0_gnn_Wq': _L0_gnn_in['Wq'], 'L0_gnn_Wk': _L0_gnn_in['Wk'], 'L0_gnn_Wv': _L0_gnn_in['Wv'], 'L0_gnn_bv': _L0_gnn_in['bv'], 'L0_gnn_Wo': _L0_gnn_in['Wo'], 'L0_gnn_bo': _L0_gnn_in['bo'], 'L1_gnn_W_left': _L1_gnn_in['W_left'], 'L1_gnn_W_right': _L1_gnn_in['W_right'], 'L1_gnn_W_lin': _L1_gnn_in['W_lin'], 'L1_gnn_b_lin': _L1_gnn_in['b_lin'], 'L1_gnn_ln_a': _L1_gnn_in['ln_a'], 'L1_gnn_ln_b': _L1_gnn_in['ln_b']}

def reference(x, adj, L0_gnn_Wq, L0_gnn_Wk, L0_gnn_Wv, L0_gnn_bv, L0_gnn_Wo, L0_gnn_bo, L1_gnn_W_left, L1_gnn_W_right, L1_gnn_W_lin, L1_gnn_b_lin, L1_gnn_ln_a, L1_gnn_ln_b):
    import jax
    import jax.numpy as jnp

    def _L0_gnn_ref(x, spatial_encoding, edge_encoding, Wq, Wk, Wv, bv, Wo, bo):
        import jax, jax.numpy as jnp
        import numpy as np
        NUM_HEADS = 12
        HIDDEN = 384
        HEAD = HIDDEN // NUM_HEADS
        B, N = (16, 256)
        b, n, h = x.shape
        scale = jnp.asarray(HIDDEN, x.dtype) ** (-0.5)
        q = (x @ Wq.T).reshape(b, n, NUM_HEADS, HEAD)
        k = (x @ Wk.T).reshape(b, n, NUM_HEADS, HEAD)
        v = (x @ Wv.T + bv).reshape(b, n, NUM_HEADS, HEAD)
        bias = (spatial_encoding + edge_encoding)[:, None]
        scores = jnp.einsum('bqhd,bkhd->bhqk', q, k) * scale + bias
        row_nonzero = jnp.any(scores != 0, axis=-1, keepdims=True)
        scores = jnp.where(row_nonzero, scores, -jnp.inf)
        p = jax.nn.softmax(scores, axis=-1)
        p = jnp.nan_to_num(p)
        out = jnp.einsum('bhqk,bkhd->bqhd', p, v).reshape(b, n, h)
        return out @ Wo.T + bo

    def _L1_gnn_ref(hidden_state, adjacency_matrix, W_left, W_right, W_lin, b_lin, ln_a, ln_b):
        import jax, jax.numpy as jnp
        import numpy as np
        B, S, H, L = (32, 256, 384, 2)

        def _layer_norm(z, a, b, eps=0.001):
            mu = jnp.mean(z, axis=-1, keepdims=True)
            sigma = jnp.std(z, axis=-1, keepdims=True, ddof=1)
            return (z - mu) / (sigma + eps) * a + b
        temper = float(np.sqrt(H))
        adj = adjacency_matrix
        adj_tri = jnp.triu(adj, k=1)
        diag_mask = jnp.triu(adj, k=0) - adj_tri
        h = hidden_state
        for l in range(L):
            m_left = jnp.einsum('bsh,oh->bso', h, W_left[l])
            m_right = jnp.einsum('bsh,oh->bso', h, W_right[l])
            u_left = jnp.einsum('bih,bjh->bij', h, m_left) / temper
            u_right = jnp.einsum('bih,bjh->bij', h, m_right) / temper
            u = u_left * adj_tri + u_left * diag_mask + u_right * jnp.swapaxes(adj_tri, 1, 2)
            delta_exp_u = jnp.exp(u) * adj
            attention = delta_exp_u / (jnp.sum(delta_exp_u, axis=2, keepdims=True) + 1e-10)
            h_lin = jnp.einsum('bsh,oh->bso', h, W_lin[l]) + b_lin[l]
            ctx = jnp.matmul(attention, h_lin)
            h = jax.nn.relu(_layer_norm(ctx, ln_a[l], ln_b[l]))
        return h
    h = jnp.maximum(_layernorm(x, axis=-1), 0.0)
    x = x + _L0_gnn_ref(h, adj, adj, L0_gnn_Wq, L0_gnn_Wk, L0_gnn_Wv, L0_gnn_bv, L0_gnn_Wo, L0_gnn_bo)
    h = jnp.maximum(_layernorm(x, axis=-1), 0.0)
    x = x + _L1_gnn_ref(h, adj, L1_gnn_W_left, L1_gnn_W_right, L1_gnn_W_lin, L1_gnn_b_lin, L1_gnn_ln_a, L1_gnn_ln_b)
    return x

_drawn_inputs = setup_inputs


def setup_inputs(seed=0):
    import zlib

    import numpy as np

    out = dict(_drawn_inputs(seed))
    spreads = {'L1_gnn_b_lin': (0.0, 0.1), 'L1_gnn_ln_a': (1.0, 0.2), 'L1_gnn_ln_b': (0.0, 0.1)}
    factors = {'L0_gnn_Wq': 8.0, 'L0_gnn_Wk': 8.0, 'L0_gnn_bv': 6.458, 'L0_gnn_bo': 2.774}
    for name, (base, spread) in spreads.items():
        noise = np.random.default_rng([zlib.crc32(name.encode()), seed]).standard_normal(out[name].shape)
        drawn = base * np.exp(spread * noise) if base else spread * noise
        out[name] = jnp.asarray(drawn.astype(out[name].dtype))
    for name, factor in factors.items():
        out[name] = (out[name] * factor).astype(out[name].dtype)
    return out
```

```python
from contextlib import ExitStack

import concourse.bass as bass
from concourse import mybir

ALU = mybir.AluOpType
ACT = mybir.ActivationFunctionType
F32 = mybir.dt.float32
F32R = mybir.dt.float32r
F16 = mybir.dt.float16
I32 = mybir.dt.int32

P = 128
H = 384
C = H // P
G = 2
T = G * P
NH = 12
D = H // NH
HC = P // D
DA = D + 1
HL = H + 2
L = 2
HI, LO = 0, 1
LN_EPS = 1e-5
GNN_EPS = 1e-3
SUM_EPS = 1e-10
Q_SCALE = H ** -0.5 / 2 * 8
K_SCALE = 1 / 8
TEMPER = H ** 0.5
RSQRT_MAGIC = 1597463007.0
WQ, WK, WV, WO = range(4)


def w_left(l):
    return 4 + 3 * l


def w_right(l):
    return 5 + 3 * l


def w_lin(l):
    return 6 + 3 * l


NW = 4 + 3 * L

A_JOBS = ["T1a", "T1b", "QK0", "QK1", "QK2", "V0", "V1", "S00", "S01", "S02", "S10", "S11", "S12",
          "P00", "P01", "P02", "PV0", "OT0", "WO0", "P10", "P11", "P12", "PV1", "OT1", "WO1",
          "T2a", "T2b"]
B_JOBS = ["AT", "N00", "N01", "N02", "HL00", "HL01", "U0", "C00", "C01", "HTa", "HTb",
          "N10", "N11", "N12", "HL10", "HL11", "U1", "C10", "C11"]
A_BANKS = 5
B_BANKS = 3
A_HI = [j for j in A_JOBS if j[0] != "S" and j[:2] not in ("PV", "WO")]
B_HI = [j for j in B_JOBS if j[0] in "NA" or j[:2] == "HL"]

ORDER = [
    ("a_ln1", 1), ("b_at", 0), ("b_n00", 0), ("b_n01", 0), ("a_t1", 1), ("b_n02", 0),
    ("a_qk0", 1), ("b_hl00", 0), ("a_qk1", 1), ("b_hl01", 0), ("a_qk2", 1), ("b_u0", 0),
    ("a_v0", 1), ("a_v1", 1), ("b_c00", 0), ("b_c01", 0), ("b_ln0", 0),
    ("a_s00", 1), ("a_s01", 1), ("a_s02", 1), ("b_ht", 0), ("a_s10", 1), ("a_s11", 1), ("a_s12", 1),
    ("a_p00", 1), ("a_p01", 1), ("a_p02", 1), ("a_pv0", 1), ("b_n10", 0), ("a_ot0", 1),
    ("b_n11", 0), ("a_wo0", 1), ("a_p10", 1), ("a_p11", 1), ("a_p12", 1), ("b_n12", 0),
    ("a_pv1", 1), ("b_hl10", 0), ("a_ot1", 1), ("b_hl11", 0), ("a_wo1", 1), ("b_u1", 0),
    ("a_ln2", 1), ("b_c10", 0), ("b_c11", 0), ("b_ln1", 0), ("a_t2", 1),
]
CONST_LOADS = 2 + 3 + 2 * C
LINKS_A = 2 * (2 + 2 + 9 + 1) + 4 * G
LINKS_B = L * (2 + 2 + 9 + 3) + L * G
AHEAD = max(ahead for _, ahead in ORDER)


def build(nc, x_d, adj_d, w_d, bias_d, bo_d, lna_d, lnb_d, out_d):
    NG = x_d.shape[0] // G
    assert x_d.shape[1] == P and x_d.shape[2] == H and NG % 2 == 0

    with ExitStack() as ctx:
        def sb(name, shape, dt=F32):
            return ctx.enter_context(nc.sbuf_tensor(name, shape, dt))

        def sem(name):
            return ctx.enter_context(nc.semaphore(name))

        banks_a = [ctx.enter_context(nc.psum_tensor(f"bank_a{i}", [P, 512], F32)) for i in range(A_BANKS)]
        banks_b = [ctx.enter_context(nc.psum_tensor(f"bank_b{i}", [P, 512], F32)) for i in range(B_BANKS)]
        full_a = [sem(f"full_a{i}") for i in range(A_BANKS)]
        free_a = [sem(f"free_a{i}") for i in range(A_BANKS)]
        full_b = [sem(f"full_b{i}") for i in range(B_BANKS)]
        free_b = [sem(f"free_b{i}") for i in range(B_BANKS)]

        W = sb("weights", [P, NW, 2, C, H], F32R)
        ident = sb("ident", [P, P])
        upper = sb("upper", [P, P])
        lower = sb("lower", [P, P])
        bias_rows = sb("bias_rows", [P, H], F32R)
        pick = sb("pick", [P, 3, P], F32R)
        bo_all = sb("bo_all", [P, H])
        lna_all = sb("lna_all", [P, H])
        lnb_all = sb("lnb_all", [P, H])
        lna_col = sb("lna_col", [P, C])
        lnb_col = sb("lnb_col", [P, C])

        x_sb = sb("x_sb", [P, 2, G, H])
        adj_sb = sb("adj_sb", [P, 2, G, P])
        hA = sb("hA", [P, 2, C, T], F32R)
        qk = sb("qk", [P, 2, 2 * C, T], F16)
        xn1 = qk[:, :, :, :].rearrange("p s c t -> p (s c t)").bitcast(F32).rearrange("p (g h) -> p g h", g=2 * G)[:, 0:G, :]
        q3 = sb("q3", [3 * D, NH, T], F16)
        k3 = sb("k3", [3 * D, NH, T], F16)
        v2 = sb("v2", [P, 2, G, NH, DA], F16)
        prob = sb("prob", [P, G, NH, P])
        pT = sb("pT", [P, 2, NH, P], F16)
        o_sb = sb("o_sb", [P, G, H])
        oT = sb("oT", [P, 2, C, P], F32R)
        x1 = sb("x1", [P, 2, G, H])
        rmax = sb("rmax", [P, G, NH])
        nmax = sb("nmax", [P, G, NH])
        row0 = sb("row0", [P, G, NH])
        rinv = sb("rinv", [P, G, NH])
        h0 = sb("h0", [P, 2, C, T], F32R)
        h1 = sb("h1", [P, 2, C, T], F32R)
        n2 = sb("n2", [P, 2, 2, C, T], F32R)
        hl = sb("hl", [P, 2, G, HL], F32R)
        work = sb("work", [P, C * T])
        tu = work[:, 0:2 * T].rearrange("p (g s i) -> p g s i", g=G, s=2)
        wu = work[:, 2 * T:3 * T].rearrange("p (g i) -> p g i", g=G)
        hx = work[:, :].rearrange("p (c t) -> p c t", c=C)
        dT = sb("dT", [P, 2, G, P], F32R)
        c_sb = sb("c_sb", [P, G, H])
        mask = sb("mask", [P, G, 2, P])
        adjT = sb("adjT", [P, G, P])

        stats = {k: sb(f"stats_{k}", [P, G, 6]) for k in ("ln1", "ln2", "gnn")}
        mv = {k: sb(f"mv_{k}", [P, G, 2]) for k in ("ln1", "ln2", "gnn")}
        newton = {k: sb(f"newton_{k}", [P, 3, G]) for k in ("ln1", "ln2", "gnn")}
        inv = {k: sb(f"inv_{k}", [P, G]) for k in ("ln1", "ln2", "gnn")}
        shift = {k: sb(f"shift_{k}", [P, G]) for k in ("ln1", "ln2", "gnn")}
        sums = sb("sums", [P, G])
        rsum = sb("rsum", [P, G])

        carrier = sb("carrier", [P, 1])

        s_wload = [sem("wload0"), sem("wload1")]
        s_setup = sem("setup")
        s_carrier = sem("carrier")
        s_whi, s_wlo, s_const, s_cload, s_gconst = (sem(n) for n in ("w_hi", "w_lo", "consts", "const_load", "gp_consts"))
        s_xin = [sem("x_in0"), sem("x_in1")]
        s_adjin = [sem("adj_in0"), sem("adj_in1")]
        s_chain_a = sem("vector_chain_a")
        s_ln1, s_xn1, s_ln2, s_xn2, s_xbo = (sem(n) for n in ("ln1_stats", "xn1", "ln2_stats", "xn2", "x_plus_bo"))
        s_hi_a = sem("hi_a")
        s_q3, s_k3 = sem("q3_in"), sem("k3_in")
        s_max, s_exp = sem("row_max"), sem("exps")
        s_chain_b = sem("vector_chain_b")
        s_hi_b = sem("hi_b")
        s_mr, s_w, s_e, s_d, s_dhi, s_dlo = (sem(n) for n in ("mask_right", "u_sum", "exp_u", "delta", "delta_hi", "delta_lo"))
        s_rsum, s_lnb, s_z, s_h1hi, s_h1lo = (sem(n) for n in ("row_sum_inv", "gnn_stats", "normed", "h1_hi", "h1_lo"))
        s_za, s_zb, s_y = sem("scaled"), sem("shifted"), sem("result")
        s_out = [sem("out0"), sem("out1")]

        hx_pick = work[:, 0:3 * P].rearrange("p (b q) -> p b q", b=3)
        ones_zeros = work[:, 3 * P:3 * P + 4 * G].rearrange("p (s g k) -> p s g k", s=2, g=G)

        def ge(eng, s, value):
            if isinstance(value, int) and value <= 0:
                return
            eng.wait_ge(s, value)

        def ring(job, stage):
            jobs, n = (A_JOBS, A_BANKS) if stage == "a" else (B_JOBS, B_BANKS)
            at = jobs.index(job)
            uses = len(range(at % n, len(jobs), n))
            return at % n, at // n, uses

        def stage_of(job):
            return "a" if job in A_JOBS else "b"

        def bank(job):
            s = stage_of(job)
            return (banks_a if s == "a" else banks_b)[ring(job, s)[0]]

        def full(job):
            s = stage_of(job)
            return (full_a if s == "a" else full_b)[ring(job, s)[0]]

        def free(job):
            s = stage_of(job)
            return (free_a if s == "a" else free_b)[ring(job, s)[0]]

        def wait_filled(eng, job, g):
            _, at, uses = ring(job, stage_of(job))
            ge(eng, full(job), uses * g + at + 1)

        def wait_drained(eng, job, g):
            _, at, uses = ring(job, stage_of(job))
            ge(eng, free(job), uses * g + at + 1)

        def wait_bank(eng, job, g):
            _, at, uses = ring(job, stage_of(job))
            ge(eng, free(job), uses * g + at)

        def wait_hi(eng, job, g):
            jobs, s = (A_HI, s_hi_a) if stage_of(job) == "a" else (B_HI, s_hi_b)
            ge(eng, s, len(jobs) * g + jobs.index(job) + 1)

        def walk(eng, run):
            def half(first, offset):
                for step, ahead in ORDER:
                    k = offset + ahead
                    if isinstance(first, int):
                        if 0 <= first + k < NG:
                            run(step, first + k, (first + k) % 2, (first + k) // 2)
                    else:
                        run(step, first * 2 + k, k % 2, first + k // 2)
            for h in range(-AHEAD, 2):
                half(h, 0)
            with eng.Fori(1, NG // 2 - 1) as pair:
                half(pair, 0)
                half(pair, 1)
            for h in range(NG - 2, NG):
                half(h, 0)

        PARTS = [(HI, HI), (HI, LO), (LO, HI)]

        block = ctx.enter_context(nc.Block())

        @block.sync
        def _(sp):
            def load(g, p):
                if isinstance(g, int) and g >= NG:
                    return
                wait_drained(sp, "WO1", g - 2)
                sp.dma_start(x_sb[:, p, :, :], x_d[bass.ds(g * G, G), :, :].rearrange("g p h -> p g h")).then_inc(s_xin[p], 16)
                ge(sp, s_mr, g - 1)
                sp.dma_start(adj_sb[:, p, :, :], adj_d[bass.ds(g * G, G), :, :].rearrange("g p h -> p g h")).then_inc(s_adjin[p], 16)

            load(0, 0)
            for m in range(NW):
                if m >= 2:
                    sp.wait_ge(s_wlo, m - 1)
                sp.dma_start(prob[:, m % 2, 0:C * C, :].rearrange("p (c a) b -> p c (a b)", c=C),
                             w_d[m].rearrange("(c p) o -> p c o", p=P)).then_inc(s_wload[m % 2], 16)

            def stack(dst, s, first, parts):
                for a in range(HC):
                    for r, part in enumerate(parts):
                        sp.dma_start(dst[D * r:D * r + D, a:NH:HC, :],
                                     qk[D * a:D * a + D, part, first:first + C, :]).then_inc(s, 16)

            def run(step, g, p, n):
                if step == "a_ln1":
                    load(g + 1, 1 - p)
                elif step == "a_qk1":
                    wait_drained(sp, "QK1", g)
                    stack(q3, s_q3, 0, (HI, LO, HI))
                elif step == "a_qk2":
                    wait_drained(sp, "QK2", g)
                    stack(k3, s_k3, C, (HI, HI, LO))
                elif step == "b_ln1":
                    ge(sp, s_y, g + 1)
                    sp.dma_start(out_d[bass.ds(g * G, G), :, :].rearrange("g p h -> p g h"), x1[:, p, :, :]).then_inc(s_out[p], 16)

            walk(sp, run)
            for p in range(2):
                sp.wait_ge(s_out[p], 16 * (NG // 2))

        STACKED = 16 * 3 * HC

        @block.tensor
        def _(pe):
            def split_mm(out, pairs, first=True, last=True):
                n = 0
                for lhsT, rhs in pairs:
                    mm = pe.matmul(out, lhsT, rhs, start=(first and n == 0), stop=(last and n == len(pairs) - 1))
                    n += 1
                return mm

            def transposes(job, g, src, chunks):
                wait_bank(pe, job, g)
                for n, c in enumerate(chunks):
                    for j in range(G):
                        mm = pe.transpose(bank(job)[:, n * T + j * P:n * T + (j + 1) * P], src[:, j, c * P:(c + 1) * P], ident[:, :])
                mm.then_inc(full(job), 1)

            def project(job, g, outs, h):
                wait_bank(pe, job, g)
                for n, (m, o) in enumerate(outs):
                    mm = split_mm(bank(job)[:, n * T:(n + 1) * T],
                                  [(W[:, m, a, c, o * P:(o + 1) * P], h[:, b, c, :]) for c in range(C) for a, b in PARTS])
                mm.then_inc(full(job), 1)

            def rows(job, g, m, h, j, bias=None):
                wait_bank(pe, job, g)
                pairs = [(h[:, a, c, j * P:(j + 1) * P], W[:, m, b, c, :]) for c in range(C) for a, b in PARTS]
                if bias is not None:
                    pairs.append((pick[:, bias, :], bias_rows[:, :]))
                split_mm(bank(job)[:, 0:H], pairs).then_inc(full(job), 1)

            def run(step, g, p, n):
                if step == "a_t1":
                    ge(pe, s_xn1, g + 1)
                    transposes("T1a", g, xn1, (0, 1))
                    transposes("T1b", g, xn1, (2,))
                elif step[:4] == "a_qk":
                    k = int(step[4])
                    if k == 0:
                        wait_drained(pe, "T1a", g)
                        wait_drained(pe, "T1b", g)
                    if k == 0 and isinstance(g, int) and g == 0:
                        pe.wait_ge(s_wlo, WK + 1)
                    outs = [(WQ, 0), (WQ, 1), (WQ, 2), (WK, 0), (WK, 1), (WK, 2)][2 * k:2 * k + 2]
                    project(f"QK{k}", g, outs, hA)
                elif step[:3] == "a_v":
                    j = int(step[3])
                    if isinstance(g, int) and g == 0:
                        pe.wait_ge(s_wlo, NW)
                        pe.wait_ge(s_const, 1)
                    rows(f"V{j}", g, WV, hA, j, bias=0)
                elif step[:3] == "a_s":
                    j, c = int(step[3]), int(step[4])
                    job = f"S{j}{c}"
                    if j == 0 and c == 0:
                        ge(pe, s_q3, STACKED * (g + 1))
                        ge(pe, s_k3, STACKED * (g + 1))
                    wait_bank(pe, job, g)
                    for a in range(HC):
                        h = c * HC + a
                        mm = pe.matmul(bank(job)[:, a * P:(a + 1) * P], q3[:, h, j * P:(j + 1) * P], k3[:, h, j * P:(j + 1) * P], start=True, stop=True)
                    mm.then_inc(full(job), 1)
                elif step[:3] == "a_p" and step[3] != "v":
                    j, c = int(step[3]), int(step[4])
                    job = f"P{j}{c}"
                    ge(pe, s_exp, G * C * g + j * C + c + 1)
                    wait_bank(pe, job, g)
                    for a in range(HC):
                        mm = pe.transpose(bank(job)[:, a * P:(a + 1) * P], prob[:, j, c * HC + a, :], ident[:, :])
                    mm.then_inc(full(job), 1)
                elif step[:4] == "a_pv":
                    j = int(step[4])
                    job = f"PV{j}"
                    if j == 0:
                        wait_drained(pe, "V0", g)
                        wait_drained(pe, "V1", g)
                    for c in range(C):
                        wait_drained(pe, f"P{j}{c}", g)
                    wait_bank(pe, job, g)
                    for h in range(NH):
                        for n, (a, b) in enumerate(PARTS):
                            mm = pe.matmul(bank(job)[:, h * DA:(h + 1) * DA], pT[:, a, h, :], v2[:, b, j, h, :],
                                           start=(h == 0 and n == 0), stop=(n == 2), skip_group_check=True)
                    mm.then_inc(full(job), 1)
                elif step[:4] == "a_ot":
                    j = int(step[4])
                    job = f"OT{j}"
                    wait_drained(pe, f"PV{j}", g)
                    wait_bank(pe, job, g)
                    for c in range(C):
                        mm = pe.transpose(bank(job)[:, c * P:(c + 1) * P], o_sb[:, j, c * P:(c + 1) * P], ident[:, :])
                    mm.then_inc(full(job), 1)
                elif step[:4] == "a_wo":
                    j = int(step[4])
                    wait_drained(pe, f"OT{j}", g)
                    rows(f"WO{j}", g, WO, oT, 0)
                elif step == "a_t2":
                    ge(pe, s_xn2, g + 1)
                    transposes("T2a", g, o_sb, (0, 1))
                    transposes("T2b", g, o_sb, (2,))
                elif step == "b_at":
                    ge(pe, s_adjin[p], 16 * (n + 1))
                    wait_bank(pe, "AT", g)
                    for j in range(G):
                        mm = pe.transpose(bank("AT")[:, j * P:(j + 1) * P], adj_sb[:, p, j, :], ident[:, :])
                    mm.then_inc(full("AT"), 1)
                elif step[:3] == "b_n":
                    l, k = int(step[3]), int(step[4])
                    if k == 0 and l == 0:
                        wait_drained(pe, "T2a", g)
                        wait_drained(pe, "T2b", g)
                    if k == 0 and l == 1:
                        ge(pe, s_h1lo, g + 1)
                    outs = [(m(l), c) for m in (w_left, w_right) for c in range(C)][2 * k:2 * k + 2]
                    project(f"N{l}{k}", g, outs, (h0, h1)[l])
                elif step[:4] == "b_hl":
                    l, j = int(step[4]), int(step[5])
                    rows(f"HL{l}{j}", g, w_lin(l), (h0, h1)[l], j, bias=1 + l)
                elif step[:3] == "b_u":
                    l = int(step[3])
                    job, h = f"U{l}", (h0, h1)[l]
                    for k in range(3):
                        wait_drained(pe, f"N{l}{k}", g)
                    wait_bank(pe, job, g)
                    for j in range(G):
                        tok = slice(j * P, (j + 1) * P)
                        mm = split_mm(bank(job)[:, j * 2 * P:(j + 1) * 2 * P],
                                      [(h[:, a, c, tok], n2[:, b, :, c, tok]) for c in range(C) for a, b in PARTS])
                    mm.then_inc(full(job), 1)
                elif step[:3] == "b_c":
                    l, j = int(step[3]), int(step[4])
                    job = f"C{l}{j}"
                    if j == 0:
                        ge(pe, s_dlo, L * g + l + 1)
                    wait_drained(pe, f"HL{l}{j}", g)
                    wait_bank(pe, job, g)
                    split_mm(bank(job)[:, 0:HL], [(dT[:, a, j, :], hl[:, b, j, :]) for a, b in PARTS]).then_inc(full(job), 1)
                elif step == "b_ht":
                    ge(pe, s_z, L * g + 1)
                    transposes("HTa", g, c_sb, (0, 1))
                    transposes("HTb", g, c_sb, (2,))

            pe.wait_ge(s_gconst, 1)
            walk(pe, run)

        @block.scalar
        def _(act):
            for m in range(NW):
                act.wait_ge(s_wload[m % 2], 16 * (m // 2 + 1))
                act.activation(W[:, m, HI, :, :], prob[:, m % 2, 0:C * C, :].rearrange("p (c a) b -> p c (a b)", c=C), ACT.Copy,
                               scale={WQ: Q_SCALE, WK: K_SCALE}.get(m, 1.0)).then_inc(s_whi, 1)
            act.wait_ge(s_cload, 16 * CONST_LOADS)

            def hi(job, grp, out, cols, pattern=None, **kw):
                wait_filled(act, job, grp)
                src = bank(job)[:, 0:cols]
                if pattern:
                    src = src.rearrange(pattern, **kw)
                act.activation(out, src, ACT.Copy).then_inc(s_hi_a if stage_of(job) == "a" else s_hi_b, 1)

            def run(step, g, p, n):
                if step == "a_ln1":
                    ge(act, s_ln1, g + 1)
                    ge(act, s_q3, STACKED * g)
                    ge(act, s_k3, STACKED * g)
                    for j in range(G):
                        z = act.activation(xn1[:, j, :], x_sb[:, p, j, :], ACT.Relu, bias=shift["ln1"][:, j:j + 1], scale=inv["ln1"][:, j:j + 1])
                    z.then_inc(s_xn1, 1)
                elif step == "a_t1":
                    hi("T1a", g, hA[:, HI, 0:2, :], 2 * T, "p (c t) -> p c t", c=2)
                    hi("T1b", g, hA[:, HI, 2, :], T)
                elif step[:4] == "a_qk":
                    k = int(step[4])
                    hi(f"QK{k}", g, qk[:, HI, 2 * k:2 * k + 2, :], 2 * T, "p (c t) -> p c t", c=2)
                elif step[:3] == "a_v":
                    j = int(step[3])
                    hi(f"V{j}", g, v2[:, HI, j, :, 0:D], H, "p (h d) -> p h d", h=NH)
                elif step[:3] == "a_s":
                    j, c = int(step[3]), int(step[4])
                    ge(act, s_max, G * C * g + j * C + c + 1)
                    for h in range(c * HC, (c + 1) * HC):
                        e = act.activation(prob[:, j, h, :], prob[:, j, h, :], ACT.Exp, bias=nmax[:, j, h:h + 1], scale=2.0)
                    e.then_inc(s_exp, 1)
                elif step[:3] == "a_p" and step[3] != "v":
                    j, c = int(step[3]), int(step[4])
                    hi(f"P{j}{c}", g, pT[:, HI, c * HC:(c + 1) * HC, :], HC * P, "p (h q) -> p h q", h=HC)
                elif step[:4] == "a_ot":
                    j = int(step[4])
                    hi(f"OT{j}", g, oT[:, HI, :, :], H, "p (c q) -> p c q", c=C)
                elif step == "a_ln2":
                    ge(act, s_ln2, g + 1)
                    for j in range(G):
                        z = act.activation(o_sb[:, j, :], x1[:, p, j, :], ACT.Relu, bias=shift["ln2"][:, j:j + 1], scale=inv["ln2"][:, j:j + 1])
                    z.then_inc(s_xn2, 1)
                elif step == "a_t2":
                    hi("T2a", g, h0[:, HI, 0:2, :], 2 * T, "p (c t) -> p c t", c=2)
                    hi("T2b", g, h0[:, HI, 2, :], T)
                elif step == "b_at":
                    hi("AT", g, adjT[:, :, :], T, "p (g i) -> p g i", g=G)
                elif step[:3] == "b_n":
                    l, k = int(step[3]), int(step[4])
                    n_flat = n2[:, HI, :, :, :].rearrange("p s c t -> p (s c) t")
                    hi(f"N{l}{k}", g, n_flat[:, 2 * k:2 * k + 2, :], 2 * T, "p (c t) -> p c t", c=2)
                elif step[:4] == "b_hl":
                    l, j = int(step[4]), int(step[5])
                    hi(f"HL{l}{j}", g, hl[:, HI, j, 0:H], H)
                elif step[:3] == "b_u":
                    l = int(step[3])
                    ge(act, s_w, L * g + l + 1)
                    act.activation(wu, wu, ACT.Exp, scale=1 / TEMPER).then_inc(s_e, 1)
                    ge(act, s_d, L * g + l + 1)
                    act.activation(dT[:, HI, :, :], wu, ACT.Copy).then_inc(s_dhi, 1)
                elif step[:3] == "b_c":
                    l, j = int(step[3]), int(step[4])
                    job = f"C{l}{j}"
                    ge(act, s_rsum, L * G * g + G * l + j + 1)
                    if l == 0:
                        ge(act, s_y, g)
                    act.activation(c_sb[:, j, :], bank(job)[:, 0:H], ACT.Copy, scale=rsum[:, j:j + 1]).then_inc(free(job), 1)
                elif step[:4] == "b_ln":
                    l = int(step[4])
                    ge(act, s_lnb, L * g + l + 1)
                    for j in range(G):
                        z = act.activation(c_sb[:, j, :], c_sb[:, j, :], ACT.Identity, bias=shift["gnn"][:, j:j + 1], scale=inv["gnn"][:, j:j + 1])
                    z.then_inc(s_z, 1)
                elif step == "b_ht":
                    for job, chunks in (("HTa", (0, 1)), ("HTb", (2,))):
                        wait_filled(act, job, g)
                        for n, c in enumerate(chunks):
                            r = act.activation(hx[:, c, :], bank(job)[:, n * T:(n + 1) * T], ACT.Relu, bias=lnb_col[:, c:c + 1], scale=lna_col[:, c:c + 1])
                        r.then_inc(free(job), 1)

            walk(act, run)

        @block.vector
        def _(dve):
            for m in range(NW):
                dve.wait_ge(s_whi, m + 1)
                dve.scalar_tensor_tensor(out=W[:, m, LO, :, :], in0=prob[:, m % 2, 0:C * C, :].rearrange("p (c a) b -> p c (a b)", c=C),
                                         scalar={WQ: Q_SCALE, WK: K_SCALE}.get(m, 1.0), in1=W[:, m, HI, :, :].bitcast(F32),
                                         op0=ALU.mult, op1=ALU.subtract).then_inc(s_wlo, 1)
            dve.wait_ge(s_cload, 16 * CONST_LOADS)
            dve.wait_ge(s_gconst, 2)
            dve.tensor_copy(bias_rows[:, :], o_sb[:, 0, :]).then_inc(s_chain_a, 1)
            dve.wait_ge(s_chain_a, 1)
            dve.tensor_tensor(o_sb[32:64, 1, :], o_sb[32:64, 0, :], bias_rows[32:64, :].bitcast(F32), ALU.subtract).then_inc(s_chain_a, 1)
            dve.wait_ge(s_chain_a, 2)
            dve.tensor_copy(bias_rows[32:64, :], o_sb[32:64, 1, :]).then_inc(s_chain_a, 1)
            dve.tensor_copy(pick[:, :, :], hx_pick).then_inc(s_chain_a, 1)
            dve.tensor_copy(hl[:, :, :, H:HL], ones_zeros).then_inc(s_chain_a, 1)
            dve.wait_ge(s_chain_a, 5)
            dve.engine_nop().then_inc(s_const, 1)
            SETUP_LINKS = 5

            links = {"a": [0, LINKS_A, SETUP_LINKS, s_chain_a], "b": [0, LINKS_B, 0, s_chain_b]}

            def link(ins, stage, g):
                k = links[stage]
                k[0] += 1
                ins.then_inc(k[3], 1)
                dve.wait_ge(k[3], k[1] * g + k[0] + k[2])

            def take_wait():
                dve.memset(carrier[:, :], 0.0).then_inc(s_carrier, 1)

            def lo(job, grp, out, hi_part, cols, pattern=None, **kw):
                wait_hi(dve, job, grp)
                src = bank(job)[:, 0:cols]
                if pattern:
                    src = src.rearrange(pattern, **kw)
                dve.tensor_tensor(out, src, hi_part if hi_part.dtype == F16 else hi_part.bitcast(F32), ALU.subtract).then_inc(free(job), 1)

            def norm_scales(k, g, stage, src, ddof_eps, done):
                for j in range(G):
                    st = dve.bn_stats(stats[k][:, j, :], src(j))
                link(st, stage, g)
                take_wait()
                for j in range(G):
                    ag = dve.bn_aggr(mv[k][:, j, :], stats[k][:, j, :])
                link(ag, stage, g)
                v, y, t = newton[k][:, 0, :], newton[k][:, 1, :], newton[k][:, 2, :]
                var, mean = mv[k][:, :, 1], mv[k][:, :, 0]
                if ddof_eps is None:
                    link(dve.tensor_scalar(v, var, LN_EPS, None, ALU.add), stage, g)
                else:
                    link(dve.tensor_scalar(v, var, H / (H - 1), None, ALU.mult), stage, g)
                link(dve.tensor_scalar(y.bitcast(I32), v.bitcast(I32), -0.5, RSQRT_MAGIC, ALU.mult, ALU.add), stage, g)
                for _ in range(3):
                    link(dve.tensor_tensor(t, y, y, ALU.mult), stage, g)
                    link(dve.scalar_tensor_tensor(out=t, in0=t, scalar=-0.5, in1=v, op0=ALU.mult, op1=ALU.mult), stage, g)
                    link(dve.scalar_tensor_tensor(out=y, in0=t, scalar=1.5, in1=y, op0=ALU.add, op1=ALU.mult), stage, g)
                if ddof_eps is None:
                    link(dve.tensor_copy(inv[k][:, :], y), stage, g)
                else:
                    link(dve.tensor_tensor(t, y, v, ALU.mult), stage, g)
                    link(dve.tensor_scalar(t, t, ddof_eps, None, ALU.add), stage, g)
                    link(dve.reciprocal(inv[k][:, :], t), stage, g)
                dve.scalar_tensor_tensor(out=shift[k][:, :], in0=mean, scalar=-1.0, in1=inv[k][:, :], op0=ALU.mult, op1=ALU.mult).then_inc(done, 1)

            def run(step, g, p, n):
                if step == "a_ln1":
                    ge(dve, s_xin[p], 16 * (n + 1))
                    norm_scales("ln1", g, "a", lambda j: x_sb[:, p, j, :], None, s_ln1)
                elif step == "a_t1":
                    lo("T1a", g, hA[:, LO, 0:2, :], hA[:, HI, 0:2, :], 2 * T, "p (c t) -> p c t", c=2)
                    lo("T1b", g, hA[:, LO, 2, :], hA[:, HI, 2, :], T)
                elif step[:4] == "a_qk":
                    k = int(step[4])
                    lo(f"QK{k}", g, qk[:, LO, 2 * k:2 * k + 2, :], qk[:, HI, 2 * k:2 * k + 2, :], 2 * T, "p (c t) -> p c t", c=2)
                elif step[:3] == "a_v":
                    j = int(step[3])
                    lo(f"V{j}", g, v2[:, LO, j, :, 0:D], v2[:, HI, j, :, 0:D], H, "p (h d) -> p h d", h=NH)
                elif step[:3] == "a_s":
                    j, c = int(step[3]), int(step[4])
                    job = f"S{j}{c}"
                    if j == 0 and c == 0:
                        ge(dve, s_adjin[p], 16 * (n + 1))
                    wait_filled(dve, job, g)
                    take_wait()
                    for a in range(HC):
                        h = c * HC + a
                        r = dve.tensor_tensor_reduce(prob[:, j, h, :], bank(job)[:, a * P:(a + 1) * P], adj_sb[:, p, j, :],
                                                     1.0, -3.0e38, ALU.add, ALU.max, rmax[:, j, h:h + 1])
                    r.then_inc(free(job), 1)
                    wait_drained(dve, job, g)
                    hs = slice(c * HC, (c + 1) * HC)
                    dve.tensor_scalar(nmax[:, j, hs], rmax[:, j, hs], -2.0, None, ALU.mult).then_inc(s_max, 1)
                elif step[:3] == "a_p" and step[3] != "v":
                    j, c = int(step[3]), int(step[4])
                    hs = slice(c * HC, (c + 1) * HC)
                    lo(f"P{j}{c}", g, pT[:, LO, hs, :], pT[:, HI, hs, :], HC * P, "p (h q) -> p h q", h=HC)
                elif step[:4] == "a_pv":
                    j = int(step[4])
                    job = f"PV{j}"
                    pv = bank(job)[:, 0:NH * DA].rearrange("p (h d) -> p h d", d=DA)
                    link(dve.tensor_scalar(row0[:, j, :], rmax[:, j, :], 0.0, None, ALU.is_equal), "a", g)
                    wait_filled(dve, job, g)
                    link(dve.scalar_tensor_tensor(out=row0[:, j, :], in0=pv[:, :, D], scalar=float(P), in1=row0[:, j, :],
                                                  op0=ALU.is_equal, op1=ALU.mult), "a", g)
                    link(dve.reciprocal(rinv[:, j, :], pv[:, :, D]), "a", g)
                    link(dve.scalar_tensor_tensor(out=rinv[:, j, :], in0=row0[:, j, :], scalar=-1.0, in1=rinv[:, j, :],
                                                  op0=ALU.add, op1=ALU.mult), "a", g)
                    dve.scalar_tensor_tensor(out=o_sb[:, j, :].rearrange("p (h d) -> p h d", h=NH), in0=pv[:, :, 0:D], scalar=-1.0,
                                             in1=rinv[:, j, :].unsqueeze(2).to_broadcast([P, NH, D]),
                                             op0=ALU.mult, op1=ALU.mult).then_inc(free(job), 1)
                elif step[:4] == "a_ot":
                    j = int(step[4])
                    lo(f"OT{j}", g, oT[:, LO, :, :], oT[:, HI, :, :], H, "p (c q) -> p c q", c=C)
                elif step[:4] == "a_wo":
                    j = int(step[4])
                    job = f"WO{j}"
                    if j == 0:
                        ge(dve, s_xbo, g + 1)
                        ge(dve, s_out[p], 16 * n)
                    wait_filled(dve, job, g)
                    dve.tensor_tensor(x1[:, p, j, :], bank(job)[:, 0:H], x_sb[:, p, j, :], ALU.add).then_inc(free(job), 1)
                elif step == "a_ln2":
                    wait_drained(dve, "WO0", g)
                    wait_drained(dve, "WO1", g)
                    norm_scales("ln2", g, "a", lambda j: x1[:, p, j, :], None, s_ln2)
                elif step == "a_t2":
                    lo("T2a", g, h0[:, LO, 0:2, :], h0[:, HI, 0:2, :], 2 * T, "p (c t) -> p c t", c=2)
                    lo("T2b", g, h0[:, LO, 2, :], h0[:, HI, 2, :], T)
                elif step == "b_at":
                    wait_hi(dve, "AT", g)
                    dve.tensor_tensor(mask[:, :, 0, :], bank("AT")[:, 0:T].rearrange("p (g i) -> p g i", g=G),
                                      upper[:, :].unsqueeze(1).to_broadcast([P, G, P]), ALU.mult).then_inc(free("AT"), 1)
                elif step[:3] == "b_n":
                    l, k = int(step[3]), int(step[4])
                    parts = [n2[:, s, :, :, :].rearrange("p s c t -> p (s c) t")[:, 2 * k:2 * k + 2, :] for s in (LO, HI)]
                    lo(f"N{l}{k}", g, parts[0], parts[1], 2 * T, "p (c t) -> p c t", c=2)
                elif step[:4] == "b_hl":
                    l, j = int(step[4]), int(step[5])
                    lo(f"HL{l}{j}", g, hl[:, LO, j, 0:H], hl[:, HI, j, 0:H], H)
                elif step[:3] == "b_u":
                    l = int(step[3])
                    job = f"U{l}"
                    if l == 0:
                        wait_drained(dve, "AT", g)
                        ge(dve, s_mr, g + 1)
                    wait_filled(dve, job, g)
                    dve.tensor_tensor(tu, bank(job)[:, :].rearrange("p (g s i) -> p g s i", g=G, s=2), mask[:, :, :, :], ALU.mult).then_inc(free(job), 1)
                elif step[:3] == "b_c":
                    l, j = int(step[3]), int(step[4])
                    job = f"C{l}{j}"
                    wait_filled(dve, job, g)
                    link(dve.tensor_scalar(sums[:, j:j + 1], bank(job)[:, H:H + 1], SUM_EPS, None, ALU.add), "b", g)
                    dve.reciprocal(rsum[:, j:j + 1], sums[:, j:j + 1]).then_inc(s_rsum, 1)
                elif step[:4] == "b_ln":
                    l = int(step[4])
                    for j in range(G):
                        wait_drained(dve, f"C{l}{j}", g)
                    norm_scales("gnn", g, "b", lambda j: c_sb[:, j, :], GNN_EPS, s_lnb)
                    if l == 1:
                        ge(dve, s_zb, g + 1)
                        flat = c_sb[:, :, :]
                        dve.scalar_tensor_tensor(out=x1[:, p, :, :], in0=flat, scalar=0.0, in1=x1[:, p, :, :],
                                                 op0=ALU.max, op1=ALU.add).then_inc(s_y, 1)
                elif step == "b_ht":
                    wait_drained(dve, "HTa", g)
                    wait_drained(dve, "HTb", g)
                    dve.tensor_copy(h1[:, HI, :, :], hx).then_inc(s_h1hi, 1)

            def walk_run(step, g, p, n):
                if step == "a_ln1":
                    links["a"][0] = 0
                if step == "b_at":
                    links["b"][0] = 0
                run(step, g, p, n)
                if step == "a_t2":
                    assert links["a"][0] == LINKS_A, links
                if step == "b_ln1":
                    assert links["b"][0] == LINKS_B, links

            walk(dve, walk_run)

        @block.gpsimd
        def _(pool):
            pool.memset(ident[:, :], 0.0).then_inc(s_setup, 1)
            pool.memset(upper[:, :], 1.0).then_inc(s_setup, 1)
            pool.memset(lower[:, :], 1.0).then_inc(s_setup, 1)
            pool.wait_ge(s_setup, 3)
            pool.affine_select(out=ident[:, :], in_=ident[:, :], compare_op=ALU.not_equal, fill=1.0, base=0,
                               pattern=[[-1, P]], channel_multiplier=1).then_inc(s_gconst, 1)
            pool.affine_select(out=upper[:, :], in_=upper[:, :], compare_op=ALU.is_ge, fill=0.0, base=0,
                               pattern=[[-1, P]], channel_multiplier=1).then_inc(s_setup, 1)
            pool.affine_select(out=lower[:, :], in_=lower[:, :], compare_op=ALU.is_ge, fill=0.0, base=-1,
                               pattern=[[1, P]], channel_multiplier=-1).then_inc(s_setup, 1)
            pool.memset(v2[:, HI, :, :, D:DA], 1.0).then_inc(s_setup, 1)
            pool.memset(v2[:, LO, :, :, D:DA], 0.0).then_inc(s_setup, 1)
            pool.memset(ones_zeros, 0.0).then_inc(s_setup, 1)
            pool.memset(hx_pick, 0.0).then_inc(s_setup, 1)
            pool.memset(o_sb[:, 0, :], 0.0).then_inc(s_setup, 1)
            pool.wait_ge(s_setup, 10)
            pool.memset(ones_zeros[:, HI, :, 0:1], 1.0).then_inc(s_setup, 1)
            for r in (0, 32):
                pool.dma_start(o_sb[r:r + 3, 0, :], bias_d).then_inc(s_cload, 16)
            for dst, src in ((bo_all[:, :], bo_d), (lna_all[:, :], lna_d[1]), (lnb_all[:, :], lnb_d[1])):
                pool.dma_start(dst, src.unsqueeze(0).to_broadcast([P, H])).then_inc(s_cload, 16)
            for dst, src in ((lna_col, lna_d[0]), (lnb_col, lnb_d[0])):
                for c in range(C):
                    pool.dma_start(dst[:, c:c + 1], src[c * P:(c + 1) * P].rearrange("(p a) -> p a", a=1)).then_inc(s_cload, 16)
            for r in (0, 32):
                for b in range(3):
                    pool.wait_ge(s_setup, 11 + (3 * r) // 32 + b)
                    pool.affine_select(out=hx_pick[:, b, :], in_=hx_pick[:, b, :], compare_op=ALU.not_equal, fill=1.0, base=-(b + r),
                                       pattern=[[0, P]], channel_multiplier=1).then_inc(s_setup, 1)
            pool.wait_ge(s_setup, 17)
            pool.wait_ge(s_cload, 16 * CONST_LOADS)
            pool.engine_nop().then_inc(s_gconst, 1)

            def run(step, g, p, n):
                if step == "a_t1":
                    ge(pool, s_xn1, g + 1)
                    pool.tensor_tensor(x_sb[:, p, :, :], x_sb[:, p, :, :], bo_all[:, :].unsqueeze(1).to_broadcast([P, G, H]), ALU.add).then_inc(s_xbo, 1)
                elif step == "b_at":
                    wait_drained(pool, "AT", g)
                    if not (isinstance(g, int) and g == 0):
                        wait_drained(pool, "U1", g - 1)
                    pool.tensor_tensor(mask[:, :, 1, :], adj_sb[:, p, :, :], lower[:, :].unsqueeze(1).to_broadcast([P, G, P]), ALU.mult).then_inc(s_mr, 1)
                elif step[:3] == "b_u":
                    l = int(step[3])
                    wait_drained(pool, f"U{l}", g)
                    pool.tensor_tensor(wu, tu[:, :, 0, :], tu[:, :, 1, :], ALU.add).then_inc(s_w, 1)
                    ge(pool, s_e, L * g + l + 1)
                    pool.tensor_tensor(wu, wu, adjT[:, :, :], ALU.mult).then_inc(s_d, 1)
                    ge(pool, s_dhi, L * g + l + 1)
                    pool.tensor_tensor(dT[:, LO, :, :], wu, dT[:, HI, :, :].bitcast(F32), ALU.subtract).then_inc(s_dlo, 1)
                elif step == "b_ht":
                    ge(pool, s_h1hi, g + 1)
                    pool.tensor_tensor(h1[:, LO, :, :], hx, h1[:, HI, :, :].bitcast(F32), ALU.subtract).then_inc(s_h1lo, 1)
                elif step == "b_ln1":
                    ge(pool, s_z, L * g + 2)
                    pool.tensor_tensor(c_sb[:, :, :], c_sb[:, :, :], lna_all[:, :].unsqueeze(1).to_broadcast([P, G, H]), ALU.mult).then_inc(s_za, 1)
                    ge(pool, s_za, g + 1)
                    pool.tensor_tensor(c_sb[:, :, :], c_sb[:, :, :], lnb_all[:, :].unsqueeze(1).to_broadcast([P, G, H]), ALU.add).then_inc(s_zb, 1)

            walk(pool, run)


def kernel(x, adj, L0_gnn_Wq, L0_gnn_Wk, L0_gnn_Wv, L0_gnn_bv, L0_gnn_Wo, L0_gnn_bo, L1_gnn_W_left, L1_gnn_W_right,
           L1_gnn_W_lin, L1_gnn_b_lin, L1_gnn_ln_a, L1_gnn_ln_b):
    import numpy as np
    import concourse.bacc as bacc
    from concourse.bass_utils import run_bass_kernel_spmd

    def rows_of(w):
        return np.ascontiguousarray(w)

    mats = [rows_of(L0_gnn_Wq).T, rows_of(L0_gnn_Wk).T, rows_of(L0_gnn_Wv).T, rows_of(L0_gnn_Wo).T]
    for l in range(L):
        mats += [rows_of(L1_gnn_W_left)[l], rows_of(L1_gnn_W_right)[l], rows_of(L1_gnn_W_lin)[l].T]
    arrays = {
        "x": rows_of(x), "adj": rows_of(adj), "w": np.ascontiguousarray(np.stack(mats)),
        "bias": np.stack([rows_of(L0_gnn_bv), rows_of(L1_gnn_b_lin)[0], rows_of(L1_gnn_b_lin)[1]]),
        "bo": rows_of(L0_gnn_bo), "lna": rows_of(L1_gnn_ln_a), "lnb": rows_of(L1_gnn_ln_b),
    }
    nc = bacc.Bacc("TRN2", target_bir_lowering=False, num_devices=1)
    args = [nc.dram_tensor(n, a.shape, mybir.dt.from_np(a.dtype), kind="ExternalInput").ap() for n, a in arrays.items()]
    out = nc.dram_tensor("out", arrays["x"].shape, F32, kind="ExternalOutput").ap()
    build(nc, *args, out)
    r = run_bass_kernel_spmd(nc, [arrays], core_ids=[0])
    return r.results[0]["out"]
```

```python
from contextlib import ExitStack

import concourse.bass as bass
from concourse import mybir

ALU = mybir.AluOpType
ACT = mybir.ActivationFunctionType
F32 = mybir.dt.float32
F32R = mybir.dt.float32r
F16 = mybir.dt.float16
I32 = mybir.dt.int32

P = 128
H = 384
C = H // P
G = 2
T = G * P
NH = 12
D = H // NH
HC = P // D
DA = D + 1
HL = H + 2
L = 2
HI, LO = 0, 1
LN_EPS = 1e-5
GNN_EPS = 1e-3
SUM_EPS = 1e-10
Q_SCALE = H ** -0.5 / 2 * 8
K_SCALE = 1 / 8
TEMPER = H ** 0.5
RSQRT_MAGIC = 1597463007.0
NEWTON = 3
WQ, WK, WV, WO = range(4)


def w_left(l):
    return 4 + 3 * l


def w_right(l):
    return 5 + 3 * l


def w_lin(l):
    return 6 + 3 * l


NW = 4 + 3 * L

RINGS = {
    "a_head": (3, [
        "T1a", "T1b", "QK0", "QK1", "QK2", "V0", "V1", "S00", "S01", "S02", "S10", "S11", "S12"]),
    "a_tail": (3, [
        "P00", "P01", "P02", "PV0", "P11", "P12", "OT0", "P10", "PV1", "WO0", "OT1", "WO1", "T2a", "T2b"]),
    "b": (2, [
        "N00", "N01", "AT", "N02", "U0", "HL00", "HL01", "C00", "C01", "HTa", "HTb", "N10", "N11", "N12", "HL10", "U1", "HL11",
        "C10", "C11"]),
}
HI_JOBS = {
    "a_head": [
        "T1a", "T1b", "QK0", "QK1", "QK2", "V0", "V1"],
    "a_tail": [
        "P00", "P01", "P02", "P11", "OT0", "P12", "P10", "OT1", "T2a", "T2b"],
    "b": [
        "N00", "N01", "AT", "N02", "HL00", "HL01", "N10", "N11", "N12", "HL10", "HL11"],
}

ORDER = {
    "SP": [
        ("b_y", -1), ("ld_x", 3), ("a_qk1", 2), ("a_qk2", 2), ("ld_adj", 2)],
    "PE": [
        ("a_s12", 1), ("b_c1", -1), ("a_p00", 1), ("a_p01", 1), ("a_p02", 1), ("b_n00", 0), ("b_n01", 0), ("b_at", 0), ("a_pv0", 1),
        ("a_p11", 1), ("b_n02", 0), ("a_p12", 1), ("a_ot0", 1), ("a_p10", 1), ("b_u0", 0), ("a_pv1", 1), ("b_hl00", 0),
        ("b_hl01", 0), ("a_wo0", 1), ("a_ot1", 1), ("a_t1", 2), ("b_c0", 0), ("a_wo1", 1), ("a_qk0", 2), ("a_qk1", 2), ("a_qk2", 2),
        ("a_v0", 2), ("b_ht", 0), ("a_v1", 2), ("a_t2", 1), ("b_n10", 0), ("b_n11", 0), ("b_n12", 0), ("b_hl10", 0), ("b_u1", 0),
        ("b_hl11", 0), ("a_s00", 2), ("a_s01", 2), ("a_s02", 2), ("a_s10", 2), ("a_s11", 2)],
    "ACT": [
        ("a_p00", 1), ("a_p01", 1), ("a_p02", 1), ("a_x12", 1), ("b_n00", 0), ("b_n01", 0), ("b_at", 0), ("b_z1", -1), ("a_p11", 1),
        ("b_n02", 0), ("a_ot0", 1), ("a_p12", 1), ("a_p10", 1), ("b_hl00", 0), ("b_e0", 0), ("a_xn1", 2), ("b_hl01", 0),
        ("a_ot1", 1), ("a_t1", 2), ("a_qk0", 2), ("a_qk1", 2), ("b_z0", 0), ("a_qk2", 2), ("a_v0", 2), ("b_ht", 0), ("a_xn2", 1),
        ("a_v1", 2), ("a_t2", 1), ("b_n10", 0), ("b_n11", 0), ("b_n12", 0), ("b_hl10", 0), ("b_e1", 0), ("b_hl11", 0), ("a_x00", 2),
        ("a_x01", 2), ("a_x02", 2), ("a_x10", 2), ("a_x11", 2), ("b_c1", 0)],
    "DVE": [
        ("a_p00", 1), ("a_p01", 1), ("b_n00", 0), ("a_p02", 1), ("gnn1_shift", -1), ("b_n01", 0), ("b_at", 0), ("a_pv0", 1),
        ("a_pn0", 1), ("a_po0", 1), ("ln1_stats", 2), ("a_p11", 1), ("ln1_aggr", 2), ("b_n02", 0), ("a_ot0", 1), ("ln1_var", 2),
        ("a_p12", 1), ("ln1_guess", 2), ("a_p10", 1), ("b_y", -1), ("b_u0", 0), ("b_w0", 0), ("a_r01", 1), ("a_pv1", 1),
        ("a_pn1", 1), ("a_po1", 1), ("ln1_shift", 2), ("b_d0", 0), ("b_dh0", 0), ("b_hl00", 0), ("b_dl0", 0), ("a_wo0", 1),
        ("b_hl01", 0), ("a_ot1", 1), ("gnn0_stats", 0), ("a_t1", 2), ("gnn0_aggr", 0), ("gnn0_var", 0), ("gnn0_guess", 0),
        ("a_wo1", 1), ("ln2_stats", 1), ("a_qk0", 2), ("ln2_aggr", 1), ("ln2_var", 1), ("a_qk1", 2), ("ln2_guess", 1),
        ("gnn0_shift", 0), ("a_qk2", 2), ("a_v0", 2), ("ln2_shift", 1), ("b_h1a", 0), ("b_l1a", 0), ("b_h1b", 0), ("b_l1b", 0),
        ("a_v1", 2), ("a_t2", 1), ("b_n10", 0), ("b_n11", 0), ("b_n12", 0), ("b_hl10", 0), ("b_u1", 0), ("b_w1", 0), ("b_d1", 0),
        ("b_dh1", 0), ("a_s00", 2), ("b_dl1", 0), ("a_s01", 2), ("a_m00", 2), ("b_hl11", 0), ("a_m01", 2), ("a_s02", 2),
        ("a_s10", 2), ("a_m02", 2), ("a_s11", 2), ("a_m10", 2), ("a_s12", 2), ("a_m11", 2), ("gnn1_stats", 0), ("a_r00", 2),
        ("gnn1_aggr", 0), ("a_m12", 2), ("gnn1_var", 0), ("gnn1_guess", 0)],
    "POOL": [
        ("gnn1", -1), ("b_at", 0), ("b_y", -1), ("ln1", 2), ("a_xbo", 2), ("gnn0", 0), ("ln2", 1)],
}
CONST_LOADS = 2 + 3 + 2 * C
AHEAD = max(ahead for steps in ORDER.values() for _, ahead in steps)
BEHIND = -min(ahead for steps in ORDER.values() for _, ahead in steps)


def build(nc, x_d, adj_d, w_d, bias_d, bo_d, lna_d, lnb_d, out_d):
    NG = x_d.shape[0] // G
    assert x_d.shape[1] == P and x_d.shape[2] == H and NG % 2 == 0

    with ExitStack() as ctx:
        def sb(name, shape, dt=F32):
            return ctx.enter_context(nc.sbuf_tensor(name, shape, dt))

        def sem(name):
            return ctx.enter_context(nc.semaphore(name))

        banks = {r: [ctx.enter_context(nc.psum_tensor(f"bank_{r}{i}", [P, 512], F32)) for i in range(n)] for r, (n, _) in RINGS.items()}
        full_sems = {r: [sem(f"full_{r}{i}") for i in range(n)] for r, (n, _) in RINGS.items()}
        free_sems = {r: [sem(f"free_{r}{i}") for i in range(n)] for r, (n, _) in RINGS.items()}
        hi_sems = {r: sem(f"hi_{r}") for r in RINGS}

        W = sb("weights", [P, NW, 2, C, H], F32R)
        ident = sb("ident", [P, P])
        upper = sb("upper", [P, P])
        lower = sb("lower", [P, P])
        bias_rows = sb("bias_rows", [P, H], F32R)
        pick = sb("pick", [P, 3, P], F32R)
        bo_all = sb("bo_all", [P, H])
        lna_all = sb("lna_all", [P, H])
        lnb_all = sb("lnb_all", [P, H])
        lna_col = sb("lna_col", [P, C])
        lnb_col = sb("lnb_col", [P, C])

        x_sb = sb("x_sb", [P, 2, G, H])
        adj_sb = sb("adj_sb", [P, 2, G, P])
        hA = sb("hA", [P, 2, C, T], F32R)
        qk = sb("qk", [P, 2, 2 * C, T], F16)
        xn1 = qk[:, :, :, :].rearrange("p s c t -> p (s c t)").bitcast(F32).rearrange("p (g h) -> p g h", g=2 * G)[:, 0:G, :]
        q3 = sb("q3", [3 * D, NH, T], F16)
        k3 = sb("k3", [3 * D, NH, T], F16)
        v2 = sb("v2", [P, 2, G, NH, DA], F16)
        prob = sb("prob", [P, G, NH, P])
        pT = sb("pT", [P, 2, NH, P], F16)
        o_sb = sb("o_sb", [P, G, H])
        oT = sb("oT", [P, 2, C, P], F32R)
        x1 = sb("x1", [P, 2, G, H])
        rmax = sb("rmax", [P, G, NH])
        nmax = sb("nmax", [P, G, NH])
        row0 = sb("row0", [P, G, NH])
        rinv = sb("rinv", [P, G, NH])
        h0 = sb("h0", [P, 2, C, T], F32R)
        h1 = sb("h1", [P, 2, C, T], F32R)
        n2 = sb("n2", [P, 2, 2, C, T], F32R)
        hl = sb("hl", [P, 2, G, HL], F32R)
        work = sb("work", [P, C * T])
        tu = work[:, 0:2 * T].rearrange("p (g s i) -> p g s i", g=G, s=2)
        wu = work[:, 2 * T:3 * T].rearrange("p (g i) -> p g i", g=G)
        hx = work[:, :].rearrange("p (c t) -> p c t", c=C)
        dT = sb("dT", [P, 2, G, P], F32R)
        c_sb = sb("c_sb", [P, G, H])
        mask = sb("mask", [P, G, 2, P])
        adjT = sb("adjT", [P, G, P])

        stats = {k: sb(f"stats_{k}", [P, G, 6]) for k in ("ln1", "ln2", "gnn")}
        mv = {k: sb(f"mv_{k}", [P, G, 2]) for k in ("ln1", "ln2", "gnn")}
        newton = {k: sb(f"newton_{k}", [P, 4, G]) for k in ("ln1", "ln2", "gnn")}
        inv = sb("inv", [P, G])
        numbers = sb("numbers", [P, 2, G])
        number = {x: numbers[:, i, :] for i, x in enumerate((-0.5, 1.5))}
        shift = {k: sb(f"shift_{k}", [P, G]) for k in ("ln1", "ln2", "gnn")}
        sums = sb("sums", [P, G])

        carrier = sb("carrier", [P, 4 + G * C])

        s_wload = [sem("wload0"), sem("wload1")]
        s_setup = sem("setup")
        s_setup_dve = sem("setup_vector")
        s_carrier = sem("carrier")
        pool_chain = {k: sem(f"pool_chain_{k}") for k in ("ln1", "ln2", "gnn")}
        s_whi, s_wlo, s_const, s_cload, s_gconst = (sem(n) for n in ("w_hi", "w_lo", "consts", "const_load", "gp_consts"))
        s_xin = [sem("x_in0"), sem("x_in1")]
        s_adjin = [sem("adj_in0"), sem("adj_in1")]
        s_ln1, s_xn1, s_ln2, s_xn2, s_xbo = (sem(n) for n in ("ln1_stats", "xn1", "ln2_stats", "xn2", "x_plus_bo"))
        s_q3, s_k3 = sem("q3_in"), sem("k3_in")
        s_max, s_exp = sem("row_max"), sem("exps")
        s_stats = {k: sem(f"stats_{k}") for k in ("ln1", "ln2", "gnn")}
        s_aggr = {k: sem(f"aggr_{k}") for k in ("ln1", "ln2", "gnn")}
        s_v = {k: sem(f"v_{k}") for k in ("ln1", "ln2", "gnn")}
        s_row0, s_recip, s_rinv, s_inv = (sem(n) for n in ("row0", "sum_inverse", "negated_inverse", "gnn_scale"))
        s_var = {k: sem(f"var_{k}") for k in ("ln1", "ln2", "gnn")}
        s_newton = {k: sem(f"newton_{k}") for k in ("ln1", "ln2", "gnn")}
        s_mr, s_w, s_e, s_d, s_dhi, s_dlo = (sem(n) for n in ("mask_right", "u_sum", "exp_u", "delta", "delta_hi", "delta_lo"))
        s_lnb, s_z, s_h1hi, s_h1lo = (sem(n) for n in ("gnn_stats", "normed", "h1_hi", "h1_lo"))
        s_za, s_zb, s_y = sem("scaled"), sem("shifted"), sem("result")
        s_out = [sem("out0"), sem("out1")]

        hx_pick = work[:, 0:3 * P].rearrange("p (b q) -> p b q", b=3)
        ones_zeros = work[:, 3 * P:3 * P + 4 * G].rearrange("p (s g k) -> p s g k", s=2, g=G)

        SPLIT_AFTER = {"t1_ready": (0, 1), "a_t1": (2,), "a_qk0": (3,), "a_qk1": (4,), "a_qk2": (5,), "a_v0": (6,), "a_v1": (7, 8, 9)}

        def staged(m):
            flat = (x1[:, :, :, :].rearrange("p k g h -> p (k g h)"),
                    pT[:, :, :, :].rearrange("p s h q -> p (s h q)").bitcast(F32))[m % 2]
            return flat[:, 0:C * H].rearrange("p (c o) -> p c o", c=C)

        def ge(eng, s, value):
            if isinstance(value, int) and value <= 0:
                return
            eng.wait_ge(s, value)

        def ring(job):
            for r, (n, jobs) in RINGS.items():
                if job in jobs:
                    at = jobs.index(job)
                    return r, at % n, at // n, len(range(at % n, len(jobs), n))

        def bank(job):
            r, at, _, _ = ring(job)
            return banks[r][at]

        def full(job):
            r, at, _, _ = ring(job)
            return full_sems[r][at]

        def free(job):
            r, at, _, _ = ring(job)
            return free_sems[r][at]

        def wait_filled(eng, job, g):
            _, _, before, uses = ring(job)
            ge(eng, full(job), uses * g + before + 1)

        def wait_drained(eng, job, g):
            _, _, before, uses = ring(job)
            ge(eng, free(job), uses * g + before + 1)

        def wait_bank(eng, job, g):
            _, _, before, uses = ring(job)
            ge(eng, free(job), uses * g + before)

        def hi_sem(job):
            return hi_sems[ring(job)[0]]

        def wait_hi(eng, job, g):
            jobs = HI_JOBS[ring(job)[0]]
            ge(eng, hi_sem(job), len(jobs) * g + jobs.index(job) + 1)

        def walk(eng, name, run):
            def half(first, offset):
                for step, ahead in ORDER[name]:
                    k = offset + ahead
                    if isinstance(first, int):
                        if 0 <= first + k < NG:
                            run(step, first + k, (first + k) % 2, (first + k) // 2)
                    else:
                        run(step, first * 2 + k, k % 2, first + k // 2)
            first = 1 + BEHIND // 2
            last = (NG - AHEAD) // 2
            for h in range(-AHEAD, 2 * first):
                half(h, 0)
            with eng.Fori(first, last) as pair:
                half(pair, 0)
                half(pair, 1)
            for h in range(2 * last, NG + BEHIND):
                half(h, 0)

        PARTS = [(HI, HI), (HI, LO), (LO, HI)]

        block = ctx.enter_context(nc.Block())

        @block.sync
        def _(sp):
            def stack(dst, s, first, parts):
                for a in range(HC):
                    for r, part in enumerate(parts):
                        sp.dma_start(dst[D * r:D * r + D, a:NH:HC, :],
                                     qk[D * a:D * a + D, part, first:first + C, :]).then_inc(s, 16)

            def run(step, g, p, n):
                if step == "ld_x":
                    wait_drained(sp, "WO1", g - 2)
                    sp.dma_start(x_sb[:, p, :, :], x_d[bass.ds(g * G, G), :, :].rearrange("g p h -> p g h")).then_inc(s_xin[p], 16)
                    if isinstance(g, int) and g == 0:
                        for m in range(NW):
                            if m >= 2:
                                sp.wait_ge(s_wlo, m - 1)
                            sp.dma_start(staged(m), w_d[m].rearrange("(c p) o -> p c o", p=P)).then_inc(s_wload[m % 2], 16)
                elif step == "ld_adj":
                    ge(sp, s_mr, g - 1)
                    sp.dma_start(adj_sb[:, p, :, :], adj_d[bass.ds(g * G, G), :, :].rearrange("g p h -> p g h")).then_inc(s_adjin[p], 16)
                elif step == "a_qk1":
                    wait_drained(sp, "QK1", g)
                    stack(q3, s_q3, 0, (HI, LO, HI))
                elif step == "a_qk2":
                    wait_drained(sp, "QK2", g)
                    stack(k3, s_k3, C, (HI, HI, LO))
                elif step == "b_y":
                    ge(sp, s_y, g + 1)
                    sp.dma_start(out_d[bass.ds(g * G, G), :, :].rearrange("g p h -> p g h"), x1[:, p, :, :]).then_inc(s_out[p], 16)

            walk(sp, "SP", run)
            for p in range(2):
                sp.wait_ge(s_out[p], 16 * (NG // 2))

        STACKED = 16 * 3 * HC

        @block.tensor
        def _(pe):
            def split_mm(out, pairs, first=True, last=True):
                n = 0
                for lhsT, rhs in pairs:
                    mm = pe.matmul(out, lhsT, rhs, start=(first and n == 0), stop=(last and n == len(pairs) - 1))
                    n += 1
                return mm

            def transposes(job, g, src, chunks):
                wait_bank(pe, job, g)
                for n, c in enumerate(chunks):
                    for j in range(G):
                        mm = pe.transpose(bank(job)[:, n * T + j * P:n * T + (j + 1) * P], src[:, j, c * P:(c + 1) * P], ident[:, :])
                mm.then_inc(full(job), 1)

            def need(m, g):
                if isinstance(g, int) and g == 0:
                    pe.wait_ge(s_wlo, m + 1)

            def project(job, g, outs, h):
                wait_bank(pe, job, g)
                need(max(m for m, _ in outs), g)
                for n, (m, o) in enumerate(outs):
                    mm = split_mm(bank(job)[:, n * T:(n + 1) * T],
                                  [(W[:, m, a, c, o * P:(o + 1) * P], h[:, b, c, :]) for c in range(C) for a, b in PARTS])
                mm.then_inc(full(job), 1)

            def rows(job, g, m, h, j, bias=None):
                wait_bank(pe, job, g)
                need(m, g)
                pairs = [(h[:, a, c, j * P:(j + 1) * P], W[:, m, b, c, :]) for c in range(C) for a, b in PARTS]
                if bias is not None:
                    pairs.append((pick[:, bias, :], bias_rows[:, :]))
                split_mm(bank(job)[:, 0:H], pairs).then_inc(full(job), 1)

            def run(step, g, p, n):
                if step == "a_t1":
                    ge(pe, s_xn1, g + 1)
                    transposes("T1a", g, xn1, (0, 1))
                    transposes("T1b", g, xn1, (2,))
                elif step[:4] == "a_qk":
                    k = int(step[4])
                    if k == 0:
                        wait_drained(pe, "T1a", g)
                        wait_drained(pe, "T1b", g)
                    outs = [(WQ, 0), (WQ, 1), (WQ, 2), (WK, 0), (WK, 1), (WK, 2)][2 * k:2 * k + 2]
                    project(f"QK{k}", g, outs, hA)
                elif step[:3] == "a_v":
                    j = int(step[3])
                    if isinstance(g, int) and g == 0:
                        pe.wait_ge(s_const, 1)
                    rows(f"V{j}", g, WV, hA, j, bias=0)
                elif step[:3] == "a_s":
                    j, c = int(step[3]), int(step[4])
                    if j == 0 and c == 0:
                        ge(pe, s_q3, STACKED * (g + 1))
                        ge(pe, s_k3, STACKED * (g + 1))
                    job = f"S{j}{c}"
                    wait_bank(pe, job, g)
                    for a in range(HC):
                        h = c * HC + a
                        mm = pe.matmul(bank(job)[:, a * P:(a + 1) * P], q3[:, h, j * P:(j + 1) * P], k3[:, h, j * P:(j + 1) * P], start=True, stop=True)
                    mm.then_inc(full(job), 1)
                elif step[:3] == "a_p" and step[3].isdigit():
                    j, c = int(step[3]), int(step[4])
                    job = f"P{j}{c}"
                    ge(pe, s_exp, G * C * g + j * C + c + 1)
                    wait_bank(pe, job, g)
                    for a in range(HC):
                        mm = pe.transpose(bank(job)[:, a * P:(a + 1) * P], prob[:, j, c * HC + a, :], ident[:, :])
                    mm.then_inc(full(job), 1)
                elif step[:4] == "a_pv":
                    j = int(step[4])
                    job = f"PV{j}"
                    if j == 0:
                        wait_drained(pe, "V0", g)
                        wait_drained(pe, "V1", g)
                    for c in range(C):
                        wait_drained(pe, f"P{j}{c}", g)
                    wait_bank(pe, job, g)
                    for h in range(NH):
                        for n, (a, b) in enumerate(PARTS):
                            mm = pe.matmul(bank(job)[:, h * DA:(h + 1) * DA], pT[:, a, h, :], v2[:, b, j, h, :],
                                           start=(h == 0 and n == 0), stop=(n == 2), skip_group_check=True)
                    mm.then_inc(full(job), 1)
                elif step[:4] == "a_ot":
                    j = int(step[4])
                    job = f"OT{j}"
                    wait_drained(pe, f"PV{j}", g)
                    wait_bank(pe, job, g)
                    for c in range(C):
                        mm = pe.transpose(bank(job)[:, c * P:(c + 1) * P], o_sb[:, j, c * P:(c + 1) * P], ident[:, :])
                    mm.then_inc(full(job), 1)
                elif step[:4] == "a_wo":
                    j = int(step[4])
                    wait_drained(pe, f"OT{j}", g)
                    rows(f"WO{j}", g, WO, oT, 0)
                elif step == "a_t2":
                    ge(pe, s_xn2, g + 1)
                    transposes("T2a", g, o_sb, (0, 1))
                    transposes("T2b", g, o_sb, (2,))
                elif step == "b_at":
                    ge(pe, s_adjin[p], 16 * (n + 1))
                    wait_bank(pe, "AT", g)
                    for j in range(G):
                        mm = pe.transpose(bank("AT")[:, j * P:(j + 1) * P], adj_sb[:, p, j, :], ident[:, :])
                    mm.then_inc(full("AT"), 1)
                elif step[:3] == "b_n":
                    l, k = int(step[3]), int(step[4])
                    if k == 0 and l == 0:
                        wait_drained(pe, "T2a", g)
                        wait_drained(pe, "T2b", g)
                    if k == 0 and l == 1:
                        ge(pe, s_h1lo, 2 * (g + 1))
                    outs = [(m(l), c) for m in (w_left, w_right) for c in range(C)][2 * k:2 * k + 2]
                    project(f"N{l}{k}", g, outs, (h0, h1)[l])
                elif step[:4] == "b_hl":
                    l, j = int(step[4]), int(step[5])
                    rows(f"HL{l}{j}", g, w_lin(l), (h0, h1)[l], j, bias=1 + l)
                elif step[:3] == "b_u":
                    l = int(step[3])
                    job, h = f"U{l}", (h0, h1)[l]
                    for k in range(3):
                        wait_drained(pe, f"N{l}{k}", g)
                    wait_bank(pe, job, g)
                    for j in range(G):
                        tok = slice(j * P, (j + 1) * P)
                        mm = split_mm(bank(job)[:, j * 2 * P:(j + 1) * 2 * P],
                                      [(h[:, a, c, tok], n2[:, b, :, c, tok]) for c in range(C) for a, b in PARTS])
                    mm.then_inc(full(job), 1)
                elif step[:3] == "b_c":
                    l = int(step[3])
                    ge(pe, s_dlo, L * g + l + 1)
                    for j in range(G):
                        job = f"C{l}{j}"
                        wait_drained(pe, f"HL{l}{j}", g)
                        wait_bank(pe, job, g)
                        split_mm(bank(job)[:, 0:HL], [(dT[:, a, j, :], hl[:, b, j, :]) for a, b in PARTS]).then_inc(full(job), 1)
                elif step == "b_ht":
                    wait_drained(pe, "C00", g)
                    wait_drained(pe, "C01", g)
                    transposes("HTa", g, c_sb, (0, 1))
                    transposes("HTb", g, c_sb, (2,))

            pe.wait_ge(s_gconst, 1)
            walk(pe, "PE", run)

        @block.scalar
        def _(act):
            def split_weights(ms):
                for m in ms:
                    act.wait_ge(s_wload[m % 2], 16 * (m // 2 + 1))
                    act.activation(W[:, m, HI, :, :], staged(m), ACT.Copy, scale={WQ: Q_SCALE, WK: K_SCALE}.get(m, 1.0)).then_inc(s_whi, 1)

            act.wait_ge(s_cload, 16 * CONST_LOADS)

            def hi(job, grp, out, cols, pattern=None, **kw):
                wait_filled(act, job, grp)
                src = bank(job)[:, 0:cols]
                if pattern:
                    src = src.rearrange(pattern, **kw)
                act.activation(out, src, ACT.Copy).then_inc(hi_sem(job), 1)

            def run(step, g, p, n):
                if step == "a_xn1":
                    ge(act, s_ln1, g + 1)
                    ge(act, s_q3, STACKED * g)
                    ge(act, s_k3, STACKED * g)
                    for j in range(G):
                        z = act.activation(xn1[:, j, :], x_sb[:, p, j, :], ACT.Relu, bias=shift["ln1"][:, j:j + 1], scale=newton["ln1"][:, 1, j:j + 1])
                    z.then_inc(s_xn1, 1)
                elif step == "a_t1":
                    hi("T1a", g, hA[:, HI, 0:2, :], 2 * T, "p (c t) -> p c t", c=2)
                    hi("T1b", g, hA[:, HI, 2, :], T)
                elif step[:4] == "a_qk":
                    k = int(step[4])
                    hi(f"QK{k}", g, qk[:, HI, 2 * k:2 * k + 2, :], 2 * T, "p (c t) -> p c t", c=2)
                elif step[:3] == "a_v":
                    j = int(step[3])
                    hi(f"V{j}", g, v2[:, HI, j, :, 0:D], H, "p (h d) -> p h d", h=NH)
                elif step[:3] == "a_x" and step != "a_xn1" and step != "a_xn2":
                    j, c = int(step[3]), int(step[4])
                    ge(act, s_max, G * C * g + j * C + c + 1)
                    for h in range(c * HC, (c + 1) * HC):
                        e = act.activation(prob[:, j, h, :], prob[:, j, h, :], ACT.Exp, bias=nmax[:, j, h:h + 1], scale=2.0)
                    e.then_inc(s_exp, 1)
                elif step[:3] == "a_p" and step[3].isdigit():
                    j, c = int(step[3]), int(step[4])
                    hi(f"P{j}{c}", g, pT[:, HI, c * HC:(c + 1) * HC, :], HC * P, "p (h q) -> p h q", h=HC)
                elif step[:4] == "a_ot":
                    j = int(step[4])
                    hi(f"OT{j}", g, oT[:, HI, :, :], H, "p (c q) -> p c q", c=C)
                elif step == "a_xn2":
                    ge(act, s_ln2, g + 1)
                    for j in range(G):
                        z = act.activation(o_sb[:, j, :], x1[:, p, j, :], ACT.Relu, bias=shift["ln2"][:, j:j + 1], scale=newton["ln2"][:, 1, j:j + 1])
                    z.then_inc(s_xn2, 1)
                elif step == "a_t2":
                    hi("T2a", g, h0[:, HI, 0:2, :], 2 * T, "p (c t) -> p c t", c=2)
                    hi("T2b", g, h0[:, HI, 2, :], T)
                elif step == "b_at":
                    hi("AT", g, adjT[:, :, :], T, "p (g i) -> p g i", g=G)
                elif step[:3] == "b_n":
                    l, k = int(step[3]), int(step[4])
                    n_flat = n2[:, HI, :, :, :].rearrange("p s c t -> p (s c) t")
                    hi(f"N{l}{k}", g, n_flat[:, 2 * k:2 * k + 2, :], 2 * T, "p (c t) -> p c t", c=2)
                elif step[:4] == "b_hl":
                    l, j = int(step[4]), int(step[5])
                    hi(f"HL{l}{j}", g, hl[:, HI, j, 0:H], H)
                elif step[:3] == "b_e":
                    l = int(step[3])
                    ge(act, s_w, L * g + l + 1)
                    act.activation(wu, wu, ACT.Exp, scale=1 / TEMPER).then_inc(s_e, 1)
                elif step[:4] == "b_dh":
                    l = int(step[4])
                    ge(act, s_d, L * g + l + 1)
                    act.activation(dT[:, HI, :, :], wu, ACT.Copy).then_inc(s_dhi, 1)
                elif step == "b_c1":
                    ge(act, s_stats["gnn"], L * g + 2)
                    for j in range(G):
                        act.activation(c_sb[:, j, :], bank(f"C1{j}")[:, 0:H], ACT.Copy).then_inc(free(f"C1{j}"), 1)
                elif step == "b_z0":
                    ge(act, s_y, g)
                    ge(act, s_lnb, L * g + 1)
                    for j in range(G):
                        act.activation(c_sb[:, j, :], bank(f"C0{j}")[:, 0:H], ACT.Identity, bias=shift["gnn"][:, j:j + 1],
                                       scale=inv[:, j:j + 1]).then_inc(free(f"C0{j}"), 1)
                elif step == "b_z1":
                    ge(act, s_lnb, L * g + 2)
                    wait_drained(act, "C10", g)
                    wait_drained(act, "C11", g)
                    for j in range(G):
                        z = act.activation(c_sb[:, j, :], c_sb[:, j, :], ACT.Identity, bias=shift["gnn"][:, j:j + 1], scale=inv[:, j:j + 1])
                    z.then_inc(s_z, 1)
                elif step == "b_ht":
                    for job, chunks in (("HTa", (0, 1)), ("HTb", (2,))):
                        wait_filled(act, job, g)
                        for n, c in enumerate(chunks):
                            r = act.activation(hx[:, c, :], bank(job)[:, n * T:(n + 1) * T], ACT.Relu, bias=lnb_col[:, c:c + 1], scale=lna_col[:, c:c + 1])
                        r.then_inc(free(job), 1)

            def run_and_split(step, g, p, n):
                run(step, g, p, n)
                if isinstance(g, int) and g == 0:
                    split_weights(SPLIT_AFTER.get({"a_xn1": "t1_ready"}.get(step, step), ()))

            walk(act, "ACT", run_and_split)

        @block.vector
        def _(dve):
            def split_weights(ms):
                for m in ms:
                    dve.wait_ge(s_whi, m + 1)
                    dve.scalar_tensor_tensor(out=W[:, m, LO, :, :], in0=staged(m), scalar={WQ: Q_SCALE, WK: K_SCALE}.get(m, 1.0),
                                             in1=W[:, m, HI, :, :].bitcast(F32), op0=ALU.mult, op1=ALU.subtract).then_inc(s_wlo, 1)

            dve.wait_ge(s_cload, 16 * CONST_LOADS)
            dve.wait_ge(s_gconst, 2)
            dve.tensor_copy(bias_rows[:, :], o_sb[:, 0, :]).then_inc(s_setup_dve, 1)
            dve.wait_ge(s_setup_dve, 1)
            dve.tensor_tensor(o_sb[32:64, 1, :], o_sb[32:64, 0, :], bias_rows[32:64, :].bitcast(F32), ALU.subtract).then_inc(s_setup_dve, 1)
            dve.wait_ge(s_setup_dve, 2)
            dve.tensor_copy(bias_rows[32:64, :], o_sb[32:64, 1, :]).then_inc(s_setup_dve, 1)
            dve.tensor_copy(pick[:, :, :], hx_pick).then_inc(s_setup_dve, 1)
            dve.tensor_copy(hl[:, :, :, H:HL], ones_zeros).then_inc(s_setup_dve, 1)
            dve.wait_ge(s_setup_dve, 5)
            dve.engine_nop().then_inc(s_const, 1)
            def take_wait(at):
                dve.memset(carrier[:, at:at + 1], 0.0).then_inc(s_carrier, 1)

            def lo(job, grp, out, hi_part, cols, pattern=None, **kw):
                wait_hi(dve, job, grp)
                src = bank(job)[:, 0:cols]
                if pattern:
                    src = src.rearrange(pattern, **kw)
                dve.tensor_tensor(out, src, hi_part if hi_part.dtype == F16 else hi_part.bitcast(F32), ALU.subtract).then_inc(free(job), 1)

            def norm(k, part, g, turn, turns, src):
                at = turns * g + turn + 1
                v, y = newton[k][:, 0, :], newton[k][:, 1, :]
                if part == "stats":
                    for j in range(G):
                        st = src(j)
                    st.then_inc(s_stats[k], 1)
                elif part == "aggr":
                    ge(dve, s_stats[k], at)
                    take_wait(("ln1", "ln2", "gnn").index(k))
                    for j in range(G):
                        ag = dve.bn_aggr(mv[k][:, j, :], stats[k][:, j, :])
                    ag.then_inc(s_aggr[k], 1)
                elif part == "var":
                    ge(dve, s_aggr[k], at)
                    op, value = (ALU.mult, H / (H - 1)) if k == "gnn" else (ALU.add, LN_EPS)
                    dve.tensor_scalar(v, mv[k][:, :, 1], value, None, op).then_inc(s_v[k], 1)
                elif part == "guess":
                    ge(dve, s_v[k], at)
                    dve.tensor_scalar(y.bitcast(I32), v.bitcast(I32), -0.5, RSQRT_MAGIC, ALU.mult, ALU.add).then_inc(s_var[k], 1)
                elif k != "gnn":
                    ge(dve, s_newton[k], at)
                    shifted(k, y, {"ln1": s_ln1, "ln2": s_ln2}[k])
                else:
                    ge(dve, s_newton[k], at)
                    dve.reciprocal(inv[:, :], newton[k][:, 2, :]).then_inc(s_inv, 1)
                    ge(dve, s_inv, at)
                    shifted(k, inv[:, :], s_lnb)

            def shifted(k, y, done):
                dve.scalar_tensor_tensor(out=shift[k][:, :], in0=mv[k][:, :, 0], scalar=-1.0, in1=y,
                                         op0=ALU.mult, op1=ALU.mult).then_inc(done, 1)

            def run(step, g, p, n):
                if step[:2] == "ln":
                    k, part = step.split("_")
                    if part == "stats" and k == "ln1":
                        ge(dve, s_xin[p], 16 * (n + 1))
                    elif part == "stats":
                        wait_drained(dve, "WO0", g)
                        wait_drained(dve, "WO1", g)
                        take_wait(3 + C * G)
                    src = x_sb if k == "ln1" else x1
                    norm(k, part, g, 0, 1, lambda j: dve.bn_stats(stats[k][:, j, :], src[:, p, j, :]))
                elif step[:3] == "gnn":
                    k, part = step.split("_")
                    l = int(k[3])

                    def bank_stats(j):
                        wait_filled(dve, f"C{l}{j}", g)
                        dve.tensor_scalar(sums[:, j:j + 1], bank(f"C{l}{j}")[:, H:H + 1], SUM_EPS, GNN_EPS, ALU.add, ALU.mult)
                        return dve.bn_stats(stats["gnn"][:, j, :], bank(f"C{l}{j}")[:, 0:H])
                    norm("gnn", part, g, l, L, bank_stats)
                elif step == "a_t1":
                    lo("T1a", g, hA[:, LO, 0:2, :], hA[:, HI, 0:2, :], 2 * T, "p (c t) -> p c t", c=2)
                    lo("T1b", g, hA[:, LO, 2, :], hA[:, HI, 2, :], T)
                elif step[:4] == "a_qk":
                    k = int(step[4])
                    lo(f"QK{k}", g, qk[:, LO, 2 * k:2 * k + 2, :], qk[:, HI, 2 * k:2 * k + 2, :], 2 * T, "p (c t) -> p c t", c=2)
                elif step[:3] == "a_v":
                    j = int(step[3])
                    lo(f"V{j}", g, v2[:, LO, j, :, 0:D], v2[:, HI, j, :, 0:D], H, "p (h d) -> p h d", h=NH)
                elif step[:3] == "a_s":
                    j, c = int(step[3]), int(step[4])
                    if j == 0 and c == 0:
                        ge(dve, s_adjin[p], 16 * (n + 1))
                    job = f"S{j}{c}"
                    wait_filled(dve, job, g)
                    take_wait(3 + j * C + c)
                    for a in range(HC):
                        h = c * HC + a
                        r = dve.tensor_tensor_reduce(prob[:, j, h, :], bank(job)[:, a * P:(a + 1) * P], adj_sb[:, p, j, :],
                                                     1.0, -3.0e38, ALU.add, ALU.max, rmax[:, j, h:h + 1])
                    r.then_inc(free(job), 1)
                elif step[:3] == "a_m":
                    j, c = int(step[3]), int(step[4])
                    wait_drained(dve, f"S{j}{c}", g)
                    hs = slice(c * HC, (c + 1) * HC)
                    dve.tensor_scalar(nmax[:, j, hs], rmax[:, j, hs], -2.0, None, ALU.mult).then_inc(s_max, 1)
                elif step[:3] == "a_p" and step[3].isdigit():
                    j, c = int(step[3]), int(step[4])
                    hs = slice(c * HC, (c + 1) * HC)
                    lo(f"P{j}{c}", g, pT[:, LO, hs, :], pT[:, HI, hs, :], HC * P, "p (h q) -> p h q", h=HC)
                elif step[:4] == "a_r0":
                    j = int(step[4])
                    dve.tensor_scalar(row0[:, j, :], rmax[:, j, :], 0.0, None, ALU.is_equal).then_inc(s_row0, 1)
                elif step[:4] in ("a_pv", "a_pn", "a_po"):
                    j = int(step[4])
                    job = f"PV{j}"
                    pv = bank(job)[:, 0:NH * DA].rearrange("p (h d) -> p h d", d=DA)
                    if step[:4] == "a_pv":
                        ge(dve, s_row0, G * g + j + 1)
                        wait_filled(dve, job, g)
                        dve.scalar_tensor_tensor(out=row0[:, j, :], in0=pv[:, :, D], scalar=float(P), in1=row0[:, j, :],
                                                 op0=ALU.is_equal, op1=ALU.mult)
                        dve.reciprocal(rinv[:, j, :], pv[:, :, D]).then_inc(s_recip, 1)
                    elif step[:4] == "a_pn":
                        ge(dve, s_recip, G * g + j + 1)
                        dve.scalar_tensor_tensor(out=rinv[:, j, :], in0=row0[:, j, :], scalar=-1.0, in1=rinv[:, j, :],
                                                 op0=ALU.add, op1=ALU.mult).then_inc(s_rinv, 1)
                    else:
                        ge(dve, s_rinv, G * g + j + 1)
                        dve.scalar_tensor_tensor(out=o_sb[:, j, :].rearrange("p (h d) -> p h d", h=NH), in0=pv[:, :, 0:D], scalar=-1.0,
                                                 in1=rinv[:, j, :].unsqueeze(2).to_broadcast([P, NH, D]),
                                                 op0=ALU.mult, op1=ALU.mult).then_inc(free(job), 1)
                elif step[:4] == "a_ot":
                    j = int(step[4])
                    lo(f"OT{j}", g, oT[:, LO, :, :], oT[:, HI, :, :], H, "p (c q) -> p c q", c=C)
                elif step[:4] == "a_wo":
                    j = int(step[4])
                    job = f"WO{j}"
                    if j == 0:
                        ge(dve, s_xbo, g + 1)
                        ge(dve, s_out[p], 16 * n)
                    wait_filled(dve, job, g)
                    dve.tensor_tensor(x1[:, p, j, :], bank(job)[:, 0:H], x_sb[:, p, j, :], ALU.add).then_inc(free(job), 1)
                elif step == "a_t2":
                    lo("T2a", g, h0[:, LO, 0:2, :], h0[:, HI, 0:2, :], 2 * T, "p (c t) -> p c t", c=2)
                    lo("T2b", g, h0[:, LO, 2, :], h0[:, HI, 2, :], T)
                elif step == "b_at":
                    wait_hi(dve, "AT", g)
                    dve.tensor_tensor(mask[:, :, 0, :], bank("AT")[:, 0:T].rearrange("p (g i) -> p g i", g=G),
                                      upper[:, :].unsqueeze(1).to_broadcast([P, G, P]), ALU.mult).then_inc(free("AT"), 1)
                elif step[:3] == "b_n":
                    l, k = int(step[3]), int(step[4])
                    parts = [n2[:, s, :, :, :].rearrange("p s c t -> p (s c) t")[:, 2 * k:2 * k + 2, :] for s in (LO, HI)]
                    lo(f"N{l}{k}", g, parts[0], parts[1], 2 * T, "p (c t) -> p c t", c=2)
                elif step[:4] == "b_hl":
                    l, j = int(step[4]), int(step[5])
                    lo(f"HL{l}{j}", g, hl[:, LO, j, 0:H], hl[:, HI, j, 0:H], H)
                elif step[:3] == "b_u":
                    l = int(step[3])
                    job = f"U{l}"
                    if l == 0:
                        wait_drained(dve, "AT", g)
                        ge(dve, s_mr, g + 1)
                    wait_filled(dve, job, g)
                    dve.tensor_tensor(tu, bank(job)[:, :].rearrange("p (g s i) -> p g s i", g=G, s=2), mask[:, :, :, :], ALU.mult).then_inc(free(job), 1)
                elif step[:3] == "b_w":
                    l = int(step[3])
                    wait_drained(dve, f"U{l}", g)
                    dve.tensor_tensor(wu, tu[:, :, 0, :], tu[:, :, 1, :], ALU.add).then_inc(s_w, 1)
                elif step[:4] == "b_dh":
                    l = int(step[4])
                    ge(dve, s_d, L * g + l + 1)
                    dve.tensor_copy(dT[:, HI, :, :], wu).then_inc(s_dhi, 1)
                elif step[:4] == "b_dl":
                    l = int(step[4])
                    ge(dve, s_dhi, L * g + l + 1)
                    dve.tensor_tensor(dT[:, LO, :, :], wu, dT[:, HI, :, :].bitcast(F32), ALU.subtract).then_inc(s_dlo, 1)
                elif step[:3] == "b_d":
                    l = int(step[3])
                    ge(dve, s_e, L * g + l + 1)
                    dve.tensor_tensor(wu, wu, adjT[:, :, :], ALU.mult).then_inc(s_d, 1)
                elif step == "b_y":
                    ge(dve, s_zb, g + 1)
                    dve.scalar_tensor_tensor(out=x1[:, p, :, :], in0=c_sb[:, :, :], scalar=0.0, in1=x1[:, p, :, :],
                                             op0=ALU.max, op1=ALU.add).then_inc(s_y, 1)
                elif step[:4] in ("b_h1", "b_l1"):
                    half = step[4]
                    cs = {"a": slice(0, 2), "b": slice(2, 3)}[half]
                    if step[2] == "h":
                        wait_drained(dve, "HT" + half, g)
                        dve.tensor_copy(h1[:, HI, cs, :], hx[:, cs, :]).then_inc(s_h1hi, 1)
                    else:
                        ge(dve, s_h1hi, 2 * g + "ab".index(half) + 1)
                        dve.tensor_tensor(h1[:, LO, cs, :], hx[:, cs, :], h1[:, HI, cs, :].bitcast(F32), ALU.subtract).then_inc(s_h1lo, 1)

            def run_and_split(step, g, p, n):
                run(step, g, p, n)
                if isinstance(g, int) and g == 0:
                    split_weights(SPLIT_AFTER.get({"ln1_shift": "t1_ready"}.get(step, step), ()))

            walk(dve, "DVE", run_and_split)

        @block.gpsimd
        def _(pool):
            pool.memset(ident[:, :], 0.0).then_inc(s_setup, 1)
            pool.memset(upper[:, :], 1.0).then_inc(s_setup, 1)
            pool.memset(lower[:, :], 1.0).then_inc(s_setup, 1)
            pool.wait_ge(s_setup, 3)
            pool.affine_select(out=ident[:, :], in_=ident[:, :], compare_op=ALU.not_equal, fill=1.0, base=0,
                               pattern=[[-1, P]], channel_multiplier=1).then_inc(s_gconst, 1)
            pool.affine_select(out=upper[:, :], in_=upper[:, :], compare_op=ALU.is_ge, fill=0.0, base=0,
                               pattern=[[-1, P]], channel_multiplier=1).then_inc(s_setup, 1)
            pool.affine_select(out=lower[:, :], in_=lower[:, :], compare_op=ALU.is_ge, fill=0.0, base=-1,
                               pattern=[[1, P]], channel_multiplier=-1).then_inc(s_setup, 1)
            pool.memset(v2[:, HI, :, :, D:DA], 1.0).then_inc(s_setup, 1)
            pool.memset(v2[:, LO, :, :, D:DA], 0.0).then_inc(s_setup, 1)
            pool.memset(ones_zeros, 0.0).then_inc(s_setup, 1)
            pool.memset(hx_pick, 0.0).then_inc(s_setup, 1)
            pool.memset(o_sb[:, 0, :], 0.0).then_inc(s_setup, 1)
            pool.wait_ge(s_setup, 10)
            pool.memset(ones_zeros[:, HI, :, 0:1], 1.0).then_inc(s_setup, 1)
            for r in (0, 32):
                pool.dma_start(o_sb[r:r + 3, 0, :], bias_d).then_inc(s_cload, 16)
            for dst, src in ((bo_all[:, :], bo_d), (lna_all[:, :], lna_d[1]), (lnb_all[:, :], lnb_d[1])):
                pool.dma_start(dst, src.unsqueeze(0).to_broadcast([P, H])).then_inc(s_cload, 16)
            for dst, src in ((lna_col, lna_d[0]), (lnb_col, lnb_d[0])):
                for c in range(C):
                    pool.dma_start(dst[:, c:c + 1], src[c * P:(c + 1) * P].rearrange("(p a) -> p a", a=1)).then_inc(s_cload, 16)
            for r in (0, 32):
                for b in range(3):
                    pool.wait_ge(s_setup, 11 + (3 * r) // 32 + b)
                    pool.affine_select(out=hx_pick[:, b, :], in_=hx_pick[:, b, :], compare_op=ALU.not_equal, fill=1.0, base=-(b + r),
                                       pattern=[[0, P]], channel_multiplier=1).then_inc(s_setup, 1)
            for x, tile in number.items():
                pool.memset(tile, x).then_inc(s_setup, 1)
            pool.wait_ge(s_setup, 19)
            pool.wait_ge(s_cload, 16 * CONST_LOADS)
            pool.engine_nop().then_inc(s_gconst, 1)

            steps = {}

            def after(ins, k, g, count):
                steps[k] = steps.get(k, 0) % count + 1
                ins.then_inc(pool_chain[k], 1)
                pool.wait_ge(pool_chain[k], count * g + steps[k])

            def rsqrt(k, g, turn=0, turns=1):
                v, y, t, half = (newton[k][:, i, :] for i in range(4))
                count = turns * (1 + 4 * NEWTON) + (turns if turns > 1 else -1)
                ge(pool, s_var[k], turns * g + turn + 1)
                after(pool.tensor_tensor(half, v, number[-0.5], ALU.mult), k, g, count)
                for i in range(NEWTON):
                    after(pool.tensor_tensor(t, y, half, ALU.mult), k, g, count)
                    after(pool.tensor_tensor(t, t, y, ALU.mult), k, g, count)
                    after(pool.tensor_tensor(t, t, number[1.5], ALU.add), k, g, count)
                    last = pool.tensor_tensor(y, y, t, ALU.mult)
                    if i < NEWTON - 1 or turns > 1:
                        after(last, k, g, count)
                if turns == 1:
                    last.then_inc(s_newton[k], 1)
                else:
                    after(pool.tensor_tensor(t, v, y, ALU.mult), k, g, count)
                    pool.tensor_tensor(t, t, sums[:, :], ALU.add).then_inc(s_newton[k], 1)

            def run(step, g, p, n):
                if step in ("ln1", "ln2"):
                    rsqrt(step, g)
                elif step[:3] == "gnn":
                    rsqrt("gnn", g, int(step[3]), L)
                elif step == "a_xbo":
                    ge(pool, s_xn1, g + 1)
                    pool.tensor_tensor(x_sb[:, p, :, :], x_sb[:, p, :, :], bo_all[:, :].unsqueeze(1).to_broadcast([P, G, H]), ALU.add).then_inc(s_xbo, 1)
                elif step == "b_at":
                    wait_drained(pool, "AT", g)
                    if not (isinstance(g, int) and g == 0):
                        wait_drained(pool, "U1", g - 1)
                    pool.tensor_tensor(mask[:, :, 1, :], adj_sb[:, p, :, :], lower[:, :].unsqueeze(1).to_broadcast([P, G, P]), ALU.mult).then_inc(s_mr, 1)
                elif step == "b_y":
                    ge(pool, s_z, g + 1)
                    pool.tensor_tensor(c_sb[:, :, :], c_sb[:, :, :], lna_all[:, :].unsqueeze(1).to_broadcast([P, G, H]), ALU.mult).then_inc(s_za, 1)
                    ge(pool, s_za, g + 1)
                    pool.tensor_tensor(c_sb[:, :, :], c_sb[:, :, :], lnb_all[:, :].unsqueeze(1).to_broadcast([P, G, H]), ALU.add).then_inc(s_zb, 1)

            walk(pool, "POOL", run)


def kernel(x, adj, L0_gnn_Wq, L0_gnn_Wk, L0_gnn_Wv, L0_gnn_bv, L0_gnn_Wo, L0_gnn_bo, L1_gnn_W_left, L1_gnn_W_right,
           L1_gnn_W_lin, L1_gnn_b_lin, L1_gnn_ln_a, L1_gnn_ln_b):
    import numpy as np
    import concourse.bacc as bacc
    from concourse.bass_utils import run_bass_kernel_spmd

    def rows_of(w):
        return np.ascontiguousarray(w)

    mats = [rows_of(L0_gnn_Wq).T, rows_of(L0_gnn_Wk).T, rows_of(L0_gnn_Wv).T, rows_of(L0_gnn_Wo).T]
    for l in range(L):
        mats += [rows_of(L1_gnn_W_left)[l], rows_of(L1_gnn_W_right)[l], rows_of(L1_gnn_W_lin)[l].T]
    arrays = {
        "x": rows_of(x), "adj": rows_of(adj), "w": np.ascontiguousarray(np.stack(mats)),
        "bias": np.stack([rows_of(L0_gnn_bv), rows_of(L1_gnn_b_lin)[0], rows_of(L1_gnn_b_lin)[1]]),
        "bo": rows_of(L0_gnn_bo), "lna": rows_of(L1_gnn_ln_a), "lnb": rows_of(L1_gnn_ln_b),
    }
    nc = bacc.Bacc("TRN2", target_bir_lowering=False, num_devices=1)
    args = [nc.dram_tensor(n, a.shape, mybir.dt.from_np(a.dtype), kind="ExternalInput").ap() for n, a in arrays.items()]
    out = nc.dram_tensor("out", arrays["x"].shape, F32, kind="ExternalOutput").ap()
    build(nc, *args, out)
    r = run_bass_kernel_spmd(nc, [arrays], core_ids=[0])
    return r.results[0]["out"]
```

```python
from contextlib import ExitStack

import concourse.bass as bass
from concourse import mybir

ALU = mybir.AluOpType
ACT = mybir.ActivationFunctionType
F32 = mybir.dt.float32
F32R = mybir.dt.float32r
F16 = mybir.dt.float16
I32 = mybir.dt.int32

P = 128
H = 384
C = H // P
G = 2
T = G * P
NH = 12
D = H // NH
HC = P // D
DA = D + 1
HL = H + 2
L = 2
HI, LO = 0, 1
LN_EPS = 1e-5
GNN_EPS = 1e-3
SUM_EPS = 1e-10
Q_SCALE = H ** -0.5 / 2 * 8
K_SCALE = 1 / 8
TEMPER = H ** 0.5
RSQRT_MAGIC = 1597463007.0
NEWTON = 3
WQ, WK, WV, WO = range(4)


def w_left(l):
    return 4 + 3 * l


def w_right(l):
    return 5 + 3 * l


def w_lin(l):
    return 6 + 3 * l


NW = 4 + 3 * L

RINGS = {
    "a_head": (3, [
        "T1a", "T1b", "QK0", "QK1", "QK2", "V0", "V1", "S00", "S01", "S11", "S10", "S02", "S12"]),
    "a_tail": (3, [
        "P00", "P01", "P02", "PV0", "P11", "P12", "P10", "OT0", "PV1", "WO0", "OT1", "WO1", "T2a", "T2b"]),
    "b": (2, [
        "AT", "N00", "N01", "N02", "U0", "HL00", "HL01", "C00", "C01", "HTa", "HTb", "N10", "N11", "N12", "HL10", "U1", "HL11",
        "C10", "C11"]),
}
HI_JOBS = {
    "a_head": [
        "T1a", "T1b", "QK0", "QK1", "QK2", "V0", "V1"],
    "a_tail": [
        "P01", "P00", "P02", "P11", "P12", "OT0", "P10", "OT1", "T2a", "T2b"],
    "b": [
        "AT", "N00", "N01", "N02", "HL00", "HL01", "N10", "N11", "N12", "HL10", "HL11"],
}

ORDER = {
    "SP": [
        ("ld_adj", 2), ("b_y", -1), ("ld_x", 3), ("a_qk1", 2), ("a_qk2", 2)],
    "PE": [
        ("b_c1", -1), ("a_p00", 1), ("a_p01", 1), ("a_s12", 1), ("b_at", 0), ("a_p02", 1), ("b_n00", 0), ("b_n01", 0), ("a_pv0", 1),
        ("a_p11", 1), ("b_n02", 0), ("a_p12", 1), ("a_p10", 1), ("a_ot0", 1), ("b_u0", 0), ("b_hl00", 0), ("a_pv1", 1),
        ("b_hl01", 0), ("a_wo0", 1), ("a_ot1", 1), ("a_t1", 2), ("b_c0", 0), ("a_wo1", 1), ("a_qk0", 2), ("a_qk1", 2), ("a_qk2", 2),
        ("a_v0", 2), ("b_ht", 0), ("a_v1", 2), ("a_t2", 1), ("b_n10", 0), ("b_n11", 0), ("b_n12", 0), ("b_hl10", 0), ("b_u1", 0),
        ("a_s00", 2), ("a_s01", 2), ("a_s11", 2), ("b_hl11", 0), ("a_s10", 2), ("a_s02", 2)],
    "ACT": [
        ("a_p01", 1), ("b_at", 0), ("a_p00", 1), ("a_x10", 1), ("b_n00", 0), ("a_p02", 1), ("a_x11", 1), ("a_x12", 1), ("b_n01", 0),
        ("a_p11", 1), ("b_z1", -1), ("b_n02", 0), ("a_p12", 1), ("a_ot0", 1), ("a_p10", 1), ("b_hl00", 0), ("b_e0", 0),
        ("a_xn1", 2), ("b_hl01", 0), ("a_ot1", 1), ("a_t1", 2), ("a_qk0", 2), ("a_qk1", 2), ("b_z0", 0), ("a_qk2", 2), ("a_v0", 2),
        ("b_ht", 0), ("a_xn2", 1), ("a_v1", 2), ("a_t2", 1), ("b_n10", 0), ("b_n11", 0), ("b_n12", 0), ("b_hl10", 0), ("b_e1", 0),
        ("b_hl11", 0), ("a_x00", 2), ("a_x01", 2), ("a_x02", 2), ("b_c1", 0)],
    "DVE": [
        ("a_m11", 1), ("a_p01", 1), ("a_s12", 1), ("a_p02", 1), ("gnn1_shift", -1), ("a_m12", 1), ("b_n00", 0), ("a_pv0", 1),
        ("a_pn0", 1), ("ln1_aggr", 2), ("ln1_var", 2), ("a_p11", 1), ("a_po0", 1), ("b_n01", 0), ("b_n02", 0), ("a_p12", 1),
        ("ln1_guess", 2), ("a_p10", 1), ("b_u0", 0), ("a_ot0", 1), ("b_w0", 0), ("b_y", -1), ("a_r01", 1), ("ln1_shift", 2),
        ("b_d0", 0), ("b_dh0", 0), ("a_pv1", 1), ("b_dl0", 0), ("b_hl00", 0), ("a_pn1", 1), ("a_po1", 1), ("b_hl01", 0),
        ("a_wo0", 1), ("a_ot1", 1), ("a_t1", 2), ("gnn0_stats", 0), ("gnn0_aggr", 0), ("gnn0_var", 0), ("gnn0_guess", 0),
        ("a_wo1", 1), ("ln2_stats", 1), ("ln2_aggr", 1), ("a_qk0", 2), ("ln2_var", 1), ("a_qk1", 2), ("gnn0_shift", 0),
        ("ln2_guess", 1), ("a_qk2", 2), ("ln2_shift", 1), ("b_h1a", 0), ("a_v0", 2), ("b_l1a", 0), ("b_h1b", 0), ("b_l1b", 0),
        ("b_n10", 0), ("b_n11", 0), ("a_t2", 1), ("b_n12", 0), ("b_hl10", 0), ("a_v1", 2), ("b_u1", 0), ("b_w1", 0), ("b_d1", 0),
        ("a_s00", 2), ("b_dh1", 0), ("a_s01", 2), ("a_m00", 2), ("b_dl1", 0), ("a_m01", 2), ("a_s11", 2), ("b_hl11", 0),
        ("a_s02", 2), ("a_m02", 2), ("gnn1_stats", 0), ("a_s10", 2), ("gnn1_aggr", 0), ("gnn1_var", 0), ("a_r00", 2),
        ("gnn1_guess", 0), ("a_m10", 2), ("ln1_stats", 3), ("b_at", 1), ("a_p00", 2)],
    "POOL": [
        ("ln2", 0), ("gnn1", -1), ("b_at", 0), ("b_y", -1), ("ln1", 2), ("a_xbo", 2), ("gnn0", 0)],
}
CONST_LOADS = 3 + 2 * C
AHEAD = max(ahead for steps in ORDER.values() for _, ahead in steps)
BEHIND = -min(ahead for steps in ORDER.values() for _, ahead in steps)


def build(nc, x_d, adj_d, w_d, bias_d, bo_d, lna_d, lnb_d, out_d):
    NG = x_d.shape[0] // G
    assert x_d.shape[1] == P and x_d.shape[2] == H and NG % 2 == 0

    with ExitStack() as ctx:
        def sb(name, shape, dt=F32):
            return ctx.enter_context(nc.sbuf_tensor(name, shape, dt))

        def sem(name):
            return ctx.enter_context(nc.semaphore(name))

        banks = {r: [ctx.enter_context(nc.psum_tensor(f"bank_{r}{i}", [P, 512], F32)) for i in range(n)] for r, (n, _) in RINGS.items()}
        full_sems = {r: [sem(f"full_{r}{i}") for i in range(n)] for r, (n, _) in RINGS.items()}
        free_sems = {r: [sem(f"free_{r}{i}") for i in range(n)] for r, (n, _) in RINGS.items()}
        hi_sems = {r: sem(f"hi_{r}") for r in RINGS}

        W = sb("weights", [P, NW, 2, C, H], F32R)
        ident = sb("ident", [P, P])
        upper = sb("upper", [P, P])
        lower = sb("lower", [P, P])
        bias_rows = sb("bias_rows", [P, H], F32R)
        pick = sb("pick", [P, 3, P], F32R)
        bo_all = sb("bo_all", [P, H])
        lna_all = sb("lna_all", [P, H])
        lnb_all = sb("lnb_all", [P, H])
        lna_col = sb("lna_col", [P, C])
        lnb_col = sb("lnb_col", [P, C])

        x_sb = sb("x_sb", [P, 2, G, H])
        adj_sb = sb("adj_sb", [P, 2, G, P])
        hA = sb("hA", [P, 2, C, T], F32R)
        qk = sb("qk", [P, 2, 2 * C, T], F16)
        xn1 = qk[:, :, :, :].rearrange("p s c t -> p (s c t)").bitcast(F32).rearrange("p (g h) -> p g h", g=2 * G)[:, 0:G, :]
        q3 = sb("q3", [3 * D, NH, T], F16)
        k3 = sb("k3", [3 * D, NH, T], F16)
        v2 = sb("v2", [P, 2, G, NH, DA], F16)
        prob = sb("prob", [P, G, NH, P])
        pT = sb("pT", [P, 2, NH, P], F16)
        o_sb = sb("o_sb", [P, G, H])
        oT = sb("oT", [P, 2, C, P], F32R)
        x1 = sb("x1", [P, 2, G, H])
        rmax = sb("rmax", [P, G, NH])
        nmax = sb("nmax", [P, G, NH])
        row0 = sb("row0", [P, G, NH])
        rinv = sb("rinv", [P, G, NH])
        h0 = sb("h0", [P, 2, C, T], F32R)
        h1 = sb("h1", [P, 2, C, T], F32R)
        n2 = sb("n2", [P, 2, 2, C, T], F32R)
        hl = sb("hl", [P, 2, G, HL], F32R)
        work = sb("work", [P, C * T])
        tu = work[:, 0:2 * T].rearrange("p (g s i) -> p g s i", g=G, s=2)
        wu = work[:, 2 * T:3 * T].rearrange("p (g i) -> p g i", g=G)
        hx = work[:, :].rearrange("p (c t) -> p c t", c=C)
        dT = sb("dT", [P, 2, G, P], F32R)
        c_sb = sb("c_sb", [P, G, H])
        mask = sb("mask", [P, G, 2, P])
        adjT = sb("adjT", [P, G, P])

        stats = {k: sb(f"stats_{k}", [P, G, 6]) for k in ("ln1", "ln2", "gnn")}
        mv = {k: sb(f"mv_{k}", [P, G, 2]) for k in ("ln1", "ln2", "gnn")}
        newton = {k: sb(f"newton_{k}", [P, 4, G]) for k in ("ln1", "ln2", "gnn")}
        inv = sb("inv", [P, G])
        three_halves = sb("three_halves", [P, G])
        shift = {k: sb(f"shift_{k}", [P, G]) for k in ("ln1", "ln2", "gnn")}
        sums = sb("sums", [P, G])

        carrier = sb("carrier", [P, 4 + G * C])

        s_wload = [sem(f"weight_in{i}") for i in range(3)]
        s_setup = sem("setup")
        s_setup_dve = sem("setup_vector")
        s_carrier = sem("carrier")
        pool_chain = {k: sem(f"pool_chain_{k}") for k in ("ln1", "ln2", "gnn")}
        s_whi, s_wlo, s_const, s_cload, s_bias, s_gconst = (sem(n) for n in ("w_hi", "w_lo", "consts", "const_load", "bias_load", "gp_consts"))
        s_xin = [sem("x_in0"), sem("x_in1")]
        s_adjin = [sem("adj_in0"), sem("adj_in1")]
        s_ln1, s_xn1, s_ln2, s_xn2, s_xbo = (sem(n) for n in ("ln1_stats", "xn1", "ln2_stats", "xn2", "x_plus_bo"))
        s_q3, s_k3 = sem("q3_in"), sem("k3_in")
        s_max, s_exp = sem("row_max"), sem("exps")
        s_stats = {k: sem(f"stats_{k}") for k in ("ln1", "ln2", "gnn")}
        s_aggr = {k: sem(f"aggr_{k}") for k in ("ln1", "ln2", "gnn")}
        s_v = {k: sem(f"v_{k}") for k in ("ln1", "ln2", "gnn")}
        s_row0, s_recip, s_rinv, s_inv = (sem(n) for n in ("row0", "sum_inverse", "negated_inverse", "gnn_scale"))
        s_var = {k: sem(f"var_{k}") for k in ("ln1", "ln2", "gnn")}
        s_newton = {k: sem(f"newton_{k}") for k in ("ln1", "ln2", "gnn")}
        s_mr, s_w, s_e, s_d, s_dhi, s_dlo = (sem(n) for n in ("mask_right", "u_sum", "exp_u", "delta", "delta_hi", "delta_lo"))
        s_lnb, s_z, s_h1hi, s_h1lo = (sem(n) for n in ("gnn_stats", "normed", "h1_hi", "h1_lo"))
        s_za, s_zb, s_y = sem("scaled"), sem("shifted"), sem("result")
        s_out = [sem("out0"), sem("out1")]

        hx_pick = work[:, 0:3 * P].rearrange("p (b q) -> p b q", b=3)
        ones_zeros = work[:, 3 * P:3 * P + 4 * G].rearrange("p (s g k) -> p s g k", s=2, g=G)

        STAGE_OF = (0, 1, 2, 0, 1, 2, 0, 1, 0, 1)
        LOAD_AFTER = {"ld_x": range(6), "a_qk2": range(6, NW)}
        SPLIT_AFTER = {"a_xn1": (0,), "ln1_shift": (0,), "a_t1": (1,), "a_qk0": (2,), "a_qk2": (3,), "a_v0": (4, 5),
                       "a_x00": range(6, NW), "a_m00": range(6, NW)}

        def staged(m):
            flat = (x1[:, :, :, :].rearrange("p k g h -> p (k g h)"),
                    pT[:, :, :, :].rearrange("p s h q -> p (s h q)").bitcast(F32),
                    prob[:, :, :, :].rearrange("p g h q -> p (g h q)"))[STAGE_OF[m]]
            return flat[:, 0:C * H].rearrange("p (c o) -> p c o", c=C)

        def load_of(m):
            return s_wload[STAGE_OF[m]], 16 * STAGE_OF[:m + 1].count(STAGE_OF[m])

        def ge(eng, s, value):
            if isinstance(value, int) and value <= 0:
                return
            eng.wait_ge(s, value)

        def ring(job):
            for r, (n, jobs) in RINGS.items():
                if job in jobs:
                    at = jobs.index(job)
                    return r, at % n, at // n, len(range(at % n, len(jobs), n))

        def bank(job):
            r, at, _, _ = ring(job)
            return banks[r][at]

        def full(job):
            r, at, _, _ = ring(job)
            return full_sems[r][at]

        def free(job):
            r, at, _, _ = ring(job)
            return free_sems[r][at]

        def wait_filled(eng, job, g):
            _, _, before, uses = ring(job)
            ge(eng, full(job), uses * g + before + 1)

        def wait_drained(eng, job, g):
            _, _, before, uses = ring(job)
            ge(eng, free(job), uses * g + before + 1)

        def wait_bank(eng, job, g):
            _, _, before, uses = ring(job)
            ge(eng, free(job), uses * g + before)

        def hi_sem(job):
            return hi_sems[ring(job)[0]]

        def wait_hi(eng, job, g):
            jobs = HI_JOBS[ring(job)[0]]
            ge(eng, hi_sem(job), len(jobs) * g + jobs.index(job) + 1)

        def walk(eng, name, run):
            def half(first, offset):
                for step, ahead in ORDER[name]:
                    k = offset + ahead
                    if isinstance(first, int):
                        if 0 <= first + k < NG:
                            run(step, first + k, (first + k) % 2, (first + k) // 2)
                    else:
                        run(step, first * 2 + k, k % 2, first + k // 2)
            first = 1 + BEHIND // 2
            last = (NG - AHEAD) // 2
            for h in range(-AHEAD, 2 * first):
                half(h, 0)
            with eng.Fori(first, last) as pair:
                half(pair, 0)
                half(pair, 1)
            for h in range(2 * last, NG + BEHIND):
                half(h, 0)

        PARTS = [(HI, HI), (HI, LO), (LO, HI)]

        block = ctx.enter_context(nc.Block())

        @block.sync
        def _(sp):
            def stack(dst, s, first, parts):
                for a in range(HC):
                    for r, part in enumerate(parts):
                        sp.dma_start(dst[D * r:D * r + D, a:NH:HC, :],
                                     qk[D * a:D * a + D, part, first:first + C, :]).then_inc(s, 16)

            def run(step, g, p, n):
                if step == "ld_x":
                    wait_drained(sp, "WO1", g - 2)
                    sp.dma_start(x_sb[:, p, :, :], x_d[bass.ds(g * G, G), :, :].rearrange("g p h -> p g h")).then_inc(s_xin[p], 16)
                elif step == "ld_adj":
                    ge(sp, s_mr, g - 1)
                    sp.dma_start(adj_sb[:, p, :, :], adj_d[bass.ds(g * G, G), :, :].rearrange("g p h -> p g h")).then_inc(s_adjin[p], 16)
                elif step == "a_qk1":
                    wait_drained(sp, "QK1", g)
                    stack(q3, s_q3, 0, (HI, LO, HI))
                elif step == "a_qk2":
                    wait_drained(sp, "QK2", g)
                    stack(k3, s_k3, C, (HI, HI, LO))
                elif step == "b_y":
                    ge(sp, s_y, g + 1)
                    sp.dma_start(out_d[bass.ds(g * G, G), :, :].rearrange("g p h -> p g h"), x1[:, p, :, :]).then_inc(s_out[p], 16)

            def run_and_load(step, g, p, n):
                run(step, g, p, n)
                if isinstance(g, int) and g == 0:
                    for m in LOAD_AFTER.get(step, ()):
                        before = [k for k in range(m) if STAGE_OF[k] == STAGE_OF[m]]
                        if before:
                            sp.wait_ge(s_wlo, before[-1] + 1)
                        sp.dma_start(staged(m), w_d[m].rearrange("(c p) o -> p c o", p=P)).then_inc(load_of(m)[0], 16)

            walk(sp, "SP", run_and_load)
            for p in range(2):
                sp.wait_ge(s_out[p], 16 * (NG // 2))

        STACKED = 16 * 3 * HC

        @block.tensor
        def _(pe):
            def split_mm(out, pairs, first=True, last=True):
                n = 0
                for lhsT, rhs in pairs:
                    mm = pe.matmul(out, lhsT, rhs, start=(first and n == 0), stop=(last and n == len(pairs) - 1))
                    n += 1
                return mm

            def transposes(job, g, src, chunks):
                wait_bank(pe, job, g)
                for n, c in enumerate(chunks):
                    for j in range(G):
                        mm = pe.transpose(bank(job)[:, n * T + j * P:n * T + (j + 1) * P], src[:, j, c * P:(c + 1) * P], ident[:, :])
                mm.then_inc(full(job), 1)

            def need(m, g):
                if isinstance(g, int) and g == 0:
                    pe.wait_ge(s_wlo, m + 1)

            def project(job, g, outs, h):
                wait_bank(pe, job, g)
                need(max(m for m, _ in outs), g)
                for n, (m, o) in enumerate(outs):
                    mm = split_mm(bank(job)[:, n * T:(n + 1) * T],
                                  [(W[:, m, a, c, o * P:(o + 1) * P], h[:, b, c, :]) for c in range(C) for a, b in PARTS])
                mm.then_inc(full(job), 1)

            def rows(job, g, m, h, j, bias=None):
                wait_bank(pe, job, g)
                need(m, g)
                pairs = [(h[:, a, c, j * P:(j + 1) * P], W[:, m, b, c, :]) for c in range(C) for a, b in PARTS]
                if bias is not None:
                    pairs.append((pick[:, bias, :], bias_rows[:, :]))
                split_mm(bank(job)[:, 0:H], pairs).then_inc(full(job), 1)

            def run(step, g, p, n):
                if step == "a_t1":
                    ge(pe, s_xn1, g + 1)
                    transposes("T1a", g, xn1, (0, 1))
                    transposes("T1b", g, xn1, (2,))
                elif step[:4] == "a_qk":
                    k = int(step[4])
                    if k == 0:
                        wait_drained(pe, "T1a", g)
                        wait_drained(pe, "T1b", g)
                    outs = [(WQ, 0), (WQ, 1), (WQ, 2), (WK, 0), (WK, 1), (WK, 2)][2 * k:2 * k + 2]
                    project(f"QK{k}", g, outs, hA)
                elif step[:3] == "a_v":
                    j = int(step[3])
                    if isinstance(g, int) and g == 0:
                        pe.wait_ge(s_const, 1)
                    rows(f"V{j}", g, WV, hA, j, bias=0)
                elif step[:3] == "a_s":
                    j, c = int(step[3]), int(step[4])
                    ge(pe, s_q3, STACKED * (g + 1))
                    ge(pe, s_k3, STACKED * (g + 1))
                    job = f"S{j}{c}"
                    wait_bank(pe, job, g)
                    for a in range(HC):
                        h = c * HC + a
                        mm = pe.matmul(bank(job)[:, a * P:(a + 1) * P], q3[:, h, j * P:(j + 1) * P], k3[:, h, j * P:(j + 1) * P], start=True, stop=True)
                    mm.then_inc(full(job), 1)
                elif step[:3] == "a_p" and step[3].isdigit():
                    j, c = int(step[3]), int(step[4])
                    job = f"P{j}{c}"
                    ge(pe, s_exp, G * C * g + j * C + c + 1)
                    wait_bank(pe, job, g)
                    for a in range(HC):
                        mm = pe.transpose(bank(job)[:, a * P:(a + 1) * P], prob[:, j, c * HC + a, :], ident[:, :])
                    mm.then_inc(full(job), 1)
                elif step[:4] == "a_pv":
                    j = int(step[4])
                    job = f"PV{j}"
                    if j == 0:
                        wait_drained(pe, "V0", g)
                        wait_drained(pe, "V1", g)
                    for c in range(C):
                        wait_drained(pe, f"P{j}{c}", g)
                    wait_bank(pe, job, g)
                    for h in range(NH):
                        for n, (a, b) in enumerate(PARTS):
                            mm = pe.matmul(bank(job)[:, h * DA:(h + 1) * DA], pT[:, a, h, :], v2[:, b, j, h, :],
                                           start=(h == 0 and n == 0), stop=(n == 2), skip_group_check=True)
                    mm.then_inc(full(job), 1)
                elif step[:4] == "a_ot":
                    j = int(step[4])
                    job = f"OT{j}"
                    wait_drained(pe, f"PV{j}", g)
                    wait_bank(pe, job, g)
                    for c in range(C):
                        mm = pe.transpose(bank(job)[:, c * P:(c + 1) * P], o_sb[:, j, c * P:(c + 1) * P], ident[:, :])
                    mm.then_inc(full(job), 1)
                elif step[:4] == "a_wo":
                    j = int(step[4])
                    wait_drained(pe, f"OT{j}", g)
                    rows(f"WO{j}", g, WO, oT, 0)
                elif step == "a_t2":
                    ge(pe, s_xn2, g + 1)
                    transposes("T2a", g, o_sb, (0, 1))
                    transposes("T2b", g, o_sb, (2,))
                elif step == "b_at":
                    ge(pe, s_adjin[p], 16 * (n + 1))
                    wait_bank(pe, "AT", g)
                    for j in range(G):
                        mm = pe.transpose(bank("AT")[:, j * P:(j + 1) * P], adj_sb[:, p, j, :], ident[:, :])
                    mm.then_inc(full("AT"), 1)
                elif step[:3] == "b_n":
                    l, k = int(step[3]), int(step[4])
                    if k == 0 and l == 0:
                        wait_drained(pe, "T2a", g)
                        wait_drained(pe, "T2b", g)
                    if k == 0 and l == 1:
                        ge(pe, s_h1lo, 2 * (g + 1))
                    outs = [(m(l), c) for m in (w_left, w_right) for c in range(C)][2 * k:2 * k + 2]
                    project(f"N{l}{k}", g, outs, (h0, h1)[l])
                elif step[:4] == "b_hl":
                    l, j = int(step[4]), int(step[5])
                    rows(f"HL{l}{j}", g, w_lin(l), (h0, h1)[l], j, bias=1 + l)
                elif step[:3] == "b_u":
                    l = int(step[3])
                    job, h = f"U{l}", (h0, h1)[l]
                    for k in range(3):
                        wait_drained(pe, f"N{l}{k}", g)
                    wait_bank(pe, job, g)
                    for j in range(G):
                        tok = slice(j * P, (j + 1) * P)
                        mm = split_mm(bank(job)[:, j * 2 * P:(j + 1) * 2 * P],
                                      [(h[:, a, c, tok], n2[:, b, :, c, tok]) for c in range(C) for a, b in PARTS])
                    mm.then_inc(full(job), 1)
                elif step[:3] == "b_c":
                    l = int(step[3])
                    ge(pe, s_dlo, L * g + l + 1)
                    for j in range(G):
                        job = f"C{l}{j}"
                        wait_drained(pe, f"HL{l}{j}", g)
                        wait_bank(pe, job, g)
                        split_mm(bank(job)[:, 0:HL], [(dT[:, a, j, :], hl[:, b, j, :]) for a, b in PARTS]).then_inc(full(job), 1)
                elif step == "b_ht":
                    wait_drained(pe, "C00", g)
                    wait_drained(pe, "C01", g)
                    transposes("HTa", g, c_sb, (0, 1))
                    transposes("HTb", g, c_sb, (2,))

            pe.wait_ge(s_gconst, 1)
            walk(pe, "PE", run)

        @block.scalar
        def _(act):
            def split_weights(ms):
                for m in ms:
                    act.wait_ge(*load_of(m))
                    act.activation(W[:, m, HI, :, :], staged(m), ACT.Copy, scale={WQ: Q_SCALE, WK: K_SCALE}.get(m, 1.0)).then_inc(s_whi, 1)

            def hi(job, grp, out, cols, pattern=None, **kw):
                wait_filled(act, job, grp)
                src = bank(job)[:, 0:cols]
                if pattern:
                    src = src.rearrange(pattern, **kw)
                act.activation(out, src, ACT.Copy).then_inc(hi_sem(job), 1)

            def run(step, g, p, n):
                if step == "a_xn1":
                    ge(act, s_ln1, g + 1)
                    ge(act, s_q3, STACKED * g)
                    ge(act, s_k3, STACKED * g)
                    for j in range(G):
                        z = act.activation(xn1[:, j, :], x_sb[:, p, j, :], ACT.Relu, bias=shift["ln1"][:, j:j + 1], scale=newton["ln1"][:, 1, j:j + 1])
                    z.then_inc(s_xn1, 1)
                elif step == "a_t1":
                    hi("T1a", g, hA[:, HI, 0:2, :], 2 * T, "p (c t) -> p c t", c=2)
                    hi("T1b", g, hA[:, HI, 2, :], T)
                elif step[:4] == "a_qk":
                    k = int(step[4])
                    hi(f"QK{k}", g, qk[:, HI, 2 * k:2 * k + 2, :], 2 * T, "p (c t) -> p c t", c=2)
                elif step[:3] == "a_v":
                    j = int(step[3])
                    hi(f"V{j}", g, v2[:, HI, j, :, 0:D], H, "p (h d) -> p h d", h=NH)
                elif step[:3] == "a_x" and step != "a_xn1" and step != "a_xn2":
                    j, c = int(step[3]), int(step[4])
                    ge(act, s_max, G * C * g + j * C + c + 1)
                    for h in range(c * HC, (c + 1) * HC):
                        e = act.activation(prob[:, j, h, :], prob[:, j, h, :], ACT.Exp, bias=nmax[:, j, h:h + 1], scale=2.0)
                    e.then_inc(s_exp, 1)
                elif step[:3] == "a_p" and step[3].isdigit():
                    j, c = int(step[3]), int(step[4])
                    hi(f"P{j}{c}", g, pT[:, HI, c * HC:(c + 1) * HC, :], HC * P, "p (h q) -> p h q", h=HC)
                elif step[:4] == "a_ot":
                    j = int(step[4])
                    hi(f"OT{j}", g, oT[:, HI, :, :], H, "p (c q) -> p c q", c=C)
                elif step == "a_xn2":
                    ge(act, s_ln2, g + 1)
                    for j in range(G):
                        z = act.activation(o_sb[:, j, :], x1[:, p, j, :], ACT.Relu, bias=shift["ln2"][:, j:j + 1], scale=newton["ln2"][:, 1, j:j + 1])
                    z.then_inc(s_xn2, 1)
                elif step == "a_t2":
                    hi("T2a", g, h0[:, HI, 0:2, :], 2 * T, "p (c t) -> p c t", c=2)
                    hi("T2b", g, h0[:, HI, 2, :], T)
                elif step == "b_at":
                    hi("AT", g, adjT[:, :, :], T, "p (g i) -> p g i", g=G)
                elif step[:3] == "b_n":
                    l, k = int(step[3]), int(step[4])
                    n_flat = n2[:, HI, :, :, :].rearrange("p s c t -> p (s c) t")
                    hi(f"N{l}{k}", g, n_flat[:, 2 * k:2 * k + 2, :], 2 * T, "p (c t) -> p c t", c=2)
                elif step[:4] == "b_hl":
                    l, j = int(step[4]), int(step[5])
                    hi(f"HL{l}{j}", g, hl[:, HI, j, 0:H], H)
                elif step[:3] == "b_e":
                    l = int(step[3])
                    ge(act, s_w, L * g + l + 1)
                    act.activation(wu, wu, ACT.Exp, scale=1 / TEMPER).then_inc(s_e, 1)
                elif step[:4] == "b_dh":
                    l = int(step[4])
                    ge(act, s_d, L * g + l + 1)
                    act.activation(dT[:, HI, :, :], wu, ACT.Copy).then_inc(s_dhi, 1)
                elif step == "b_c1":
                    ge(act, s_stats["gnn"], L * g + 2)
                    for j in range(G):
                        act.activation(c_sb[:, j, :], bank(f"C1{j}")[:, 0:H], ACT.Copy).then_inc(free(f"C1{j}"), 1)
                elif step == "b_z0":
                    ge(act, s_y, g)
                    ge(act, s_lnb, L * g + 1)
                    for j in range(G):
                        act.activation(c_sb[:, j, :], bank(f"C0{j}")[:, 0:H], ACT.Identity, bias=shift["gnn"][:, j:j + 1],
                                       scale=inv[:, j:j + 1]).then_inc(free(f"C0{j}"), 1)
                elif step == "b_z1":
                    ge(act, s_lnb, L * g + 2)
                    wait_drained(act, "C10", g)
                    wait_drained(act, "C11", g)
                    for j in range(G):
                        z = act.activation(c_sb[:, j, :], c_sb[:, j, :], ACT.Identity, bias=shift["gnn"][:, j:j + 1], scale=inv[:, j:j + 1])
                    z.then_inc(s_z, 1)
                elif step == "b_ht":
                    if isinstance(g, int) and g == 0:
                        act.wait_ge(s_cload, 16 * CONST_LOADS)
                    for job, chunks in (("HTa", (0, 1)), ("HTb", (2,))):
                        wait_filled(act, job, g)
                        for n, c in enumerate(chunks):
                            r = act.activation(hx[:, c, :], bank(job)[:, n * T:(n + 1) * T], ACT.Relu, bias=lnb_col[:, c:c + 1], scale=lna_col[:, c:c + 1])
                        r.then_inc(free(job), 1)

            def run_and_split(step, g, p, n):
                run(step, g, p, n)
                if isinstance(g, int) and g == 0:
                    split_weights(SPLIT_AFTER.get(step, ()))

            walk(act, "ACT", run_and_split)

        @block.vector
        def _(dve):
            def split_weights(ms):
                for m in ms:
                    dve.wait_ge(s_whi, m + 1)
                    dve.scalar_tensor_tensor(out=W[:, m, LO, :, :], in0=staged(m), scalar={WQ: Q_SCALE, WK: K_SCALE}.get(m, 1.0),
                                             in1=W[:, m, HI, :, :].bitcast(F32), op0=ALU.mult, op1=ALU.subtract).then_inc(s_wlo, 1)

            def make_constants():
                dve.wait_ge(s_bias, 32)
                dve.wait_ge(s_gconst, 2)
                dve.tensor_copy(bias_rows[:, :], o_sb[:, 0, :]).then_inc(s_setup_dve, 1)
                dve.wait_ge(s_setup_dve, 1)
                dve.tensor_tensor(o_sb[32:64, 1, :], o_sb[32:64, 0, :], bias_rows[32:64, :].bitcast(F32), ALU.subtract).then_inc(s_setup_dve, 1)
                dve.wait_ge(s_setup_dve, 2)
                dve.tensor_copy(bias_rows[32:64, :], o_sb[32:64, 1, :]).then_inc(s_setup_dve, 1)
                dve.tensor_copy(pick[:, :, :], hx_pick).then_inc(s_setup_dve, 1)
                dve.tensor_copy(hl[:, :, :, H:HL], ones_zeros).then_inc(s_setup_dve, 1)
                dve.wait_ge(s_setup_dve, 5)
                dve.engine_nop().then_inc(s_const, 1)
            def take_wait(at):
                dve.memset(carrier[:, at:at + 1], 0.0).then_inc(s_carrier, 1)

            def lo(job, grp, out, hi_part, cols, pattern=None, **kw):
                wait_hi(dve, job, grp)
                src = bank(job)[:, 0:cols]
                if pattern:
                    src = src.rearrange(pattern, **kw)
                dve.tensor_tensor(out, src, hi_part if hi_part.dtype == F16 else hi_part.bitcast(F32), ALU.subtract).then_inc(free(job), 1)

            def norm(k, part, g, turn, turns, src):
                at = turns * g + turn + 1
                v, y = newton[k][:, 0, :], newton[k][:, 1, :]
                if part == "stats":
                    for j in range(G):
                        st = src(j)
                    st.then_inc(s_stats[k], 1)
                elif part == "aggr":
                    ge(dve, s_stats[k], at)
                    take_wait(("ln1", "ln2", "gnn").index(k))
                    for j in range(G):
                        ag = dve.bn_aggr(mv[k][:, j, :], stats[k][:, j, :])
                    ag.then_inc(s_aggr[k], 1)
                elif part == "var":
                    ge(dve, s_aggr[k], at)
                    op, value = (ALU.mult, H / (H - 1)) if k == "gnn" else (ALU.add, LN_EPS)
                    dve.tensor_scalar(v, mv[k][:, :, 1], value, None, op).then_inc(s_v[k], 1)
                elif part == "guess":
                    ge(dve, s_v[k], at)
                    dve.tensor_scalar(newton[k][:, 3, :], v, -0.5, None, ALU.mult)
                    dve.tensor_scalar(y.bitcast(I32), v.bitcast(I32), -0.5, RSQRT_MAGIC, ALU.mult, ALU.add).then_inc(s_var[k], 1)
                elif k != "gnn":
                    ge(dve, s_newton[k], at)
                    shifted(k, y, {"ln1": s_ln1, "ln2": s_ln2}[k])
                else:
                    ge(dve, s_newton[k], at)
                    dve.reciprocal(inv[:, :], newton[k][:, 2, :]).then_inc(s_inv, 1)
                    ge(dve, s_inv, at)
                    shifted(k, inv[:, :], s_lnb)

            def shifted(k, y, done):
                dve.scalar_tensor_tensor(out=shift[k][:, :], in0=mv[k][:, :, 0], scalar=-1.0, in1=y,
                                         op0=ALU.mult, op1=ALU.mult).then_inc(done, 1)

            def run(step, g, p, n):
                if step[:2] == "ln":
                    k, part = step.split("_")
                    if part == "stats" and k == "ln1":
                        ge(dve, s_xin[p], 16 * (n + 1))
                    elif part == "stats":
                        wait_drained(dve, "WO0", g)
                        wait_drained(dve, "WO1", g)
                        take_wait(3 + C * G)
                    src = x_sb if k == "ln1" else x1
                    norm(k, part, g, 0, 1, lambda j: dve.bn_stats(stats[k][:, j, :], src[:, p, j, :]))
                elif step[:3] == "gnn":
                    k, part = step.split("_")
                    l = int(k[3])

                    def bank_stats(j):
                        wait_filled(dve, f"C{l}{j}", g)
                        dve.tensor_scalar(sums[:, j:j + 1], bank(f"C{l}{j}")[:, H:H + 1], SUM_EPS, GNN_EPS, ALU.add, ALU.mult)
                        return dve.bn_stats(stats["gnn"][:, j, :], bank(f"C{l}{j}")[:, 0:H])
                    norm("gnn", part, g, l, L, bank_stats)
                elif step == "a_t1":
                    lo("T1a", g, hA[:, LO, 0:2, :], hA[:, HI, 0:2, :], 2 * T, "p (c t) -> p c t", c=2)
                    lo("T1b", g, hA[:, LO, 2, :], hA[:, HI, 2, :], T)
                elif step[:4] == "a_qk":
                    k = int(step[4])
                    lo(f"QK{k}", g, qk[:, LO, 2 * k:2 * k + 2, :], qk[:, HI, 2 * k:2 * k + 2, :], 2 * T, "p (c t) -> p c t", c=2)
                elif step[:3] == "a_v":
                    j = int(step[3])
                    lo(f"V{j}", g, v2[:, LO, j, :, 0:D], v2[:, HI, j, :, 0:D], H, "p (h d) -> p h d", h=NH)
                elif step[:3] == "a_s":
                    j, c = int(step[3]), int(step[4])
                    if j == 0 and c == 0:
                        ge(dve, s_adjin[p], 16 * (n + 1))
                        if isinstance(g, int) and g == 0:
                            dve.wait_ge(s_wlo, 1 + max(m for m in range(NW) if STAGE_OF[m] == 2))
                    job = f"S{j}{c}"
                    wait_filled(dve, job, g)
                    take_wait(3 + j * C + c)
                    for a in range(HC):
                        h = c * HC + a
                        r = dve.tensor_tensor_reduce(prob[:, j, h, :], bank(job)[:, a * P:(a + 1) * P], adj_sb[:, p, j, :],
                                                     1.0, -3.0e38, ALU.add, ALU.max, rmax[:, j, h:h + 1])
                    r.then_inc(free(job), 1)
                elif step[:3] == "a_m":
                    j, c = int(step[3]), int(step[4])
                    wait_drained(dve, f"S{j}{c}", g)
                    hs = slice(c * HC, (c + 1) * HC)
                    dve.tensor_scalar(nmax[:, j, hs], rmax[:, j, hs], -2.0, None, ALU.mult).then_inc(s_max, 1)
                elif step[:3] == "a_p" and step[3].isdigit():
                    j, c = int(step[3]), int(step[4])
                    hs = slice(c * HC, (c + 1) * HC)
                    lo(f"P{j}{c}", g, pT[:, LO, hs, :], pT[:, HI, hs, :], HC * P, "p (h q) -> p h q", h=HC)
                elif step[:4] == "a_r0":
                    j = int(step[4])
                    dve.tensor_scalar(row0[:, j, :], rmax[:, j, :], 0.0, None, ALU.is_equal).then_inc(s_row0, 1)
                elif step[:4] in ("a_pv", "a_pn", "a_po"):
                    j = int(step[4])
                    job = f"PV{j}"
                    pv = bank(job)[:, 0:NH * DA].rearrange("p (h d) -> p h d", d=DA)
                    if step[:4] == "a_pv":
                        ge(dve, s_row0, G * g + j + 1)
                        wait_filled(dve, job, g)
                        dve.scalar_tensor_tensor(out=row0[:, j, :], in0=pv[:, :, D], scalar=float(P), in1=row0[:, j, :],
                                                 op0=ALU.is_equal, op1=ALU.mult)
                        dve.reciprocal(rinv[:, j, :], pv[:, :, D]).then_inc(s_recip, 1)
                    elif step[:4] == "a_pn":
                        ge(dve, s_recip, G * g + j + 1)
                        dve.scalar_tensor_tensor(out=rinv[:, j, :], in0=row0[:, j, :], scalar=-1.0, in1=rinv[:, j, :],
                                                 op0=ALU.add, op1=ALU.mult).then_inc(s_rinv, 1)
                    else:
                        ge(dve, s_rinv, G * g + j + 1)
                        dve.scalar_tensor_tensor(out=o_sb[:, j, :].rearrange("p (h d) -> p h d", h=NH), in0=pv[:, :, 0:D], scalar=-1.0,
                                                 in1=rinv[:, j, :].unsqueeze(2).to_broadcast([P, NH, D]),
                                                 op0=ALU.mult, op1=ALU.mult).then_inc(free(job), 1)
                elif step[:4] == "a_ot":
                    j = int(step[4])
                    lo(f"OT{j}", g, oT[:, LO, :, :], oT[:, HI, :, :], H, "p (c q) -> p c q", c=C)
                elif step[:4] == "a_wo":
                    j = int(step[4])
                    job = f"WO{j}"
                    if j == 0:
                        ge(dve, s_xbo, g + 1)
                        ge(dve, s_out[p], 16 * n)
                    wait_filled(dve, job, g)
                    dve.tensor_tensor(x1[:, p, j, :], bank(job)[:, 0:H], x_sb[:, p, j, :], ALU.add).then_inc(free(job), 1)
                elif step == "a_t2":
                    lo("T2a", g, h0[:, LO, 0:2, :], h0[:, HI, 0:2, :], 2 * T, "p (c t) -> p c t", c=2)
                    lo("T2b", g, h0[:, LO, 2, :], h0[:, HI, 2, :], T)
                elif step == "b_at":
                    wait_hi(dve, "AT", g)
                    dve.tensor_tensor(mask[:, :, 0, :], bank("AT")[:, 0:T].rearrange("p (g i) -> p g i", g=G),
                                      upper[:, :].unsqueeze(1).to_broadcast([P, G, P]), ALU.mult).then_inc(free("AT"), 1)
                elif step[:3] == "b_n":
                    l, k = int(step[3]), int(step[4])
                    parts = [n2[:, s, :, :, :].rearrange("p s c t -> p (s c) t")[:, 2 * k:2 * k + 2, :] for s in (LO, HI)]
                    lo(f"N{l}{k}", g, parts[0], parts[1], 2 * T, "p (c t) -> p c t", c=2)
                elif step[:4] == "b_hl":
                    l, j = int(step[4]), int(step[5])
                    lo(f"HL{l}{j}", g, hl[:, LO, j, 0:H], hl[:, HI, j, 0:H], H)
                elif step[:3] == "b_u":
                    l = int(step[3])
                    job = f"U{l}"
                    if l == 0:
                        wait_drained(dve, "AT", g)
                        ge(dve, s_mr, g + 1)
                    wait_filled(dve, job, g)
                    dve.tensor_tensor(tu, bank(job)[:, :].rearrange("p (g s i) -> p g s i", g=G, s=2), mask[:, :, :, :], ALU.mult).then_inc(free(job), 1)
                elif step[:3] == "b_w":
                    l = int(step[3])
                    wait_drained(dve, f"U{l}", g)
                    dve.tensor_tensor(wu, tu[:, :, 0, :], tu[:, :, 1, :], ALU.add).then_inc(s_w, 1)
                elif step[:4] == "b_dh":
                    l = int(step[4])
                    ge(dve, s_d, L * g + l + 1)
                    dve.tensor_copy(dT[:, HI, :, :], wu).then_inc(s_dhi, 1)
                elif step[:4] == "b_dl":
                    l = int(step[4])
                    ge(dve, s_dhi, L * g + l + 1)
                    dve.tensor_tensor(dT[:, LO, :, :], wu, dT[:, HI, :, :].bitcast(F32), ALU.subtract).then_inc(s_dlo, 1)
                elif step[:3] == "b_d":
                    l = int(step[3])
                    ge(dve, s_e, L * g + l + 1)
                    dve.tensor_tensor(wu, wu, adjT[:, :, :], ALU.mult).then_inc(s_d, 1)
                elif step == "b_y":
                    ge(dve, s_zb, g + 1)
                    dve.scalar_tensor_tensor(out=x1[:, p, :, :], in0=c_sb[:, :, :], scalar=0.0, in1=x1[:, p, :, :],
                                             op0=ALU.max, op1=ALU.add).then_inc(s_y, 1)
                elif step[:4] in ("b_h1", "b_l1"):
                    half = step[4]
                    cs = {"a": slice(0, 2), "b": slice(2, 3)}[half]
                    if step[2] == "h":
                        wait_drained(dve, "HT" + half, g)
                        dve.tensor_copy(h1[:, HI, cs, :], hx[:, cs, :]).then_inc(s_h1hi, 1)
                    else:
                        ge(dve, s_h1hi, 2 * g + "ab".index(half) + 1)
                        dve.tensor_tensor(h1[:, LO, cs, :], hx[:, cs, :], h1[:, HI, cs, :].bitcast(F32), ALU.subtract).then_inc(s_h1lo, 1)

            def run_and_split(step, g, p, n):
                run(step, g, p, n)
                if isinstance(g, int) and g == 0:
                    split_weights(SPLIT_AFTER.get(step, ()))
                    if step == "a_qk1":
                        make_constants()

            walk(dve, "DVE", run_and_split)

        @block.gpsimd
        def _(pool):
            pool.memset(ident[:, :], 0.0).then_inc(s_setup, 1)
            pool.memset(three_halves[:, :], 1.5).then_inc(s_setup, 1)
            pool.wait_ge(s_setup, 2)
            pool.affine_select(out=ident[:, :], in_=ident[:, :], compare_op=ALU.not_equal, fill=1.0, base=0,
                               pattern=[[-1, P]], channel_multiplier=1).then_inc(s_gconst, 1)

            def make_constants():
                pool.memset(o_sb[:, 0, :], 0.0).then_inc(s_setup, 1)
                pool.wait_ge(s_setup, 3)
                for r in (0, 32):
                    pool.dma_start(o_sb[r:r + 3, 0, :], bias_d).then_inc(s_bias, 16)
                for dst, src in ((bo_all[:, :], bo_d), (lna_all[:, :], lna_d[1]), (lnb_all[:, :], lnb_d[1])):
                    pool.dma_start(dst, src.unsqueeze(0).to_broadcast([P, H])).then_inc(s_cload, 16)
                for dst, src in ((lna_col, lna_d[0]), (lnb_col, lnb_d[0])):
                    for c in range(C):
                        pool.dma_start(dst[:, c:c + 1], src[c * P:(c + 1) * P].rearrange("(p a) -> p a", a=1)).then_inc(s_cload, 16)
                pool.memset(v2[:, HI, :, :, D:DA], 1.0).then_inc(s_setup, 1)
                pool.memset(v2[:, LO, :, :, D:DA], 0.0).then_inc(s_setup, 1)
                pool.memset(ones_zeros, 0.0).then_inc(s_setup, 1)
                pool.memset(hx_pick, 0.0).then_inc(s_setup, 1)
                pool.memset(upper[:, :], 1.0).then_inc(s_setup, 1)
                pool.memset(lower[:, :], 1.0).then_inc(s_setup, 1)
                pool.wait_ge(s_setup, 9)
                pool.memset(ones_zeros[:, HI, :, 0:1], 1.0).then_inc(s_setup, 1)
                pool.affine_select(out=upper[:, :], in_=upper[:, :], compare_op=ALU.is_ge, fill=0.0, base=0,
                                   pattern=[[-1, P]], channel_multiplier=1).then_inc(s_setup, 1)
                pool.affine_select(out=lower[:, :], in_=lower[:, :], compare_op=ALU.is_ge, fill=0.0, base=-1,
                                   pattern=[[1, P]], channel_multiplier=-1).then_inc(s_setup, 1)
                for r in (0, 32):
                    for b in range(3):
                        pool.wait_ge(s_setup, 12 + (3 * r) // 32 + b)
                        pool.affine_select(out=hx_pick[:, b, :], in_=hx_pick[:, b, :], compare_op=ALU.not_equal, fill=1.0, base=-(b + r),
                                           pattern=[[0, P]], channel_multiplier=1).then_inc(s_setup, 1)
                pool.wait_ge(s_setup, 18)
                pool.engine_nop().then_inc(s_gconst, 1)
                pool.wait_ge(s_cload, 16 * CONST_LOADS)

            place = {}

            def link(ins, k):
                place[k] = place.get(k, 0) + 1
                ins.then_inc(pool_chain[k], 1)

            def wait_links(k, before):
                pool.wait_ge(pool_chain[k], before + place[k])

            def rsqrt(k, g, turn=0):
                v, y, t, half = (newton[k][:, i, :] for i in range(4))
                gnn = k == "gnn"
                links = 4 * NEWTON + (1 if gnn else -1)
                before = links * ((L * g + turn) if gnn else g)
                place[k] = 0
                ge(pool, s_var[k], (L * g + turn if gnn else g) + 1)
                for i in range(NEWTON):
                    final = gnn and i == NEWTON - 1
                    link(pool.tensor_tensor(t, y, half, ALU.mult), k)
                    wait_links(k, before)
                    if final:
                        link(pool.tensor_tensor(v, v, y, ALU.mult), k)
                    link(pool.tensor_tensor(t, t, y, ALU.mult), k)
                    wait_links(k, before)
                    link(pool.tensor_tensor(t, t, three_halves[:, :], ALU.add), k)
                    wait_links(k, before)
                    if final:
                        link(pool.tensor_tensor(t, t, v, ALU.mult), k)
                        wait_links(k, before)
                        pool.tensor_tensor(t, t, sums[:, :], ALU.add).then_inc(s_newton[k], 1)
                    elif i == NEWTON - 1:
                        pool.tensor_tensor(y, y, t, ALU.mult).then_inc(s_newton[k], 1)
                    else:
                        link(pool.tensor_tensor(y, y, t, ALU.mult), k)
                        wait_links(k, before)
                assert place[k] == links

            def run(step, g, p, n):
                if step in ("ln1", "ln2"):
                    rsqrt(step, g)
                    if step == "ln1" and isinstance(g, int) and g == 0:
                        make_constants()
                elif step[:3] == "gnn":
                    rsqrt("gnn", g, int(step[3]))
                elif step == "a_xbo":
                    ge(pool, s_xn1, g + 1)
                    pool.tensor_tensor(x_sb[:, p, :, :], x_sb[:, p, :, :], bo_all[:, :].unsqueeze(1).to_broadcast([P, G, H]), ALU.add).then_inc(s_xbo, 1)
                elif step == "b_at":
                    wait_drained(pool, "AT", g)
                    if not (isinstance(g, int) and g == 0):
                        wait_drained(pool, "U1", g - 1)
                    pool.tensor_tensor(mask[:, :, 1, :], adj_sb[:, p, :, :], lower[:, :].unsqueeze(1).to_broadcast([P, G, P]), ALU.mult).then_inc(s_mr, 1)
                elif step == "b_y":
                    ge(pool, s_z, g + 1)
                    pool.tensor_tensor(c_sb[:, :, :], c_sb[:, :, :], lna_all[:, :].unsqueeze(1).to_broadcast([P, G, H]), ALU.mult).then_inc(s_za, 1)
                    ge(pool, s_za, g + 1)
                    pool.tensor_tensor(c_sb[:, :, :], c_sb[:, :, :], lnb_all[:, :].unsqueeze(1).to_broadcast([P, G, H]), ALU.add).then_inc(s_zb, 1)

            walk(pool, "POOL", run)


def kernel(x, adj, L0_gnn_Wq, L0_gnn_Wk, L0_gnn_Wv, L0_gnn_bv, L0_gnn_Wo, L0_gnn_bo, L1_gnn_W_left, L1_gnn_W_right,
           L1_gnn_W_lin, L1_gnn_b_lin, L1_gnn_ln_a, L1_gnn_ln_b):
    import numpy as np
    import concourse.bacc as bacc
    from concourse.bass_utils import run_bass_kernel_spmd

    def rows_of(w):
        return np.ascontiguousarray(w)

    mats = [rows_of(L0_gnn_Wq).T, rows_of(L0_gnn_Wk).T, rows_of(L0_gnn_Wv).T, rows_of(L0_gnn_Wo).T]
    for l in range(L):
        mats += [rows_of(L1_gnn_W_left)[l], rows_of(L1_gnn_W_right)[l], rows_of(L1_gnn_W_lin)[l].T]
    arrays = {
        "x": rows_of(x), "adj": rows_of(adj), "w": np.ascontiguousarray(np.stack(mats)),
        "bias": np.stack([rows_of(L0_gnn_bv), rows_of(L1_gnn_b_lin)[0], rows_of(L1_gnn_b_lin)[1]]),
        "bo": rows_of(L0_gnn_bo), "lna": rows_of(L1_gnn_ln_a), "lnb": rows_of(L1_gnn_ln_b),
    }
    nc = bacc.Bacc("TRN2", target_bir_lowering=False, num_devices=1)
    args = [nc.dram_tensor(n, a.shape, mybir.dt.from_np(a.dtype), kind="ExternalInput").ap() for n, a in arrays.items()]
    out = nc.dram_tensor("out", arrays["x"].shape, F32, kind="ExternalOutput").ap()
    build(nc, *args, out)
    r = run_bass_kernel_spmd(nc, [arrays], core_ids=[0])
    return r.results[0]["out"]
```
